# Optimizing a Trainium2 kernel written in Bass

```python
import numpy as np
import jax
import jax.numpy as jnp

def _softmax(x, axis=-1):
    return jax.nn.softmax(x, axis=axis)

def _gelu(x):
    return jax.nn.gelu(x, approximate=True)

def _silu(x):
    return jax.nn.silu(x)

def _sigmoid(x):
    return jax.nn.sigmoid(x)

def _layernorm(x, axis=-1, eps=1e-05):
    m = jnp.mean(x, axis=axis, keepdims=True)
    v = jnp.var(x, axis=axis, keepdims=True)
    return (x - m) / jnp.sqrt(v + eps)

def _scatter_add(tgt, idx, src, axis=0):
    return tgt.at[idx].add(src)

def _segment_sum(src, seg, n):
    return jax.ops.segment_sum(src, seg, n)
kernel_name = 'mk_gnn_resnorm_d2_gnn_r8_5ea9e6'

def setup_inputs(seed: int=0):
    np.random.seed(seed)
    _w = jnp.asarray

    def _rec_inputs():
        import jax
        import jax.numpy as jnp
        _gk = jax.random.key(seed)
        x = -0.000202 + 1 * jax.random.normal(jax.random.fold_in(_gk, 1), (12500, 64), jnp.float32)
        src = jax.random.randint(jax.random.fold_in(_gk, 2), (400000,), 0, 12500, jnp.int32)
        dst = jax.random.randint(jax.random.fold_in(_gk, 3), (400000,), 0, 12500, jnp.int32)
        _o = jnp.argsort(dst, stable=True)
        src = src[_o]
        dst = dst[_o]
        return (x, src, dst)
    x, src, dst = _rec_inputs()

    def _L0_gnn_setup():
        import jax, jax.numpy as jnp
        import numpy as np
        N_NODES = 12500
        N_EDGES = 200000
        IN_DIM = 64
        OUT_DIM = 64
        BN_EPS = 1e-05
        LRELU_SLOPE = 0.3
        key = jax.random.key(seed)
        k1, k2, k3, k4, k5, k6 = jax.random.split(key, 6)
        feature = jax.random.normal(k1, (N_NODES, IN_DIM), dtype=jnp.float32)
        edge_index = jax.random.randint(k2, (2, N_EDGES), 0, N_NODES, dtype=jnp.int32)
        lim = 1.0 / np.sqrt(2 * IN_DIM)
        W = jax.random.uniform(k3, (OUT_DIM, 2 * IN_DIM), jnp.float32, -lim, lim)
        b = jax.random.uniform(k4, (OUT_DIM,), jnp.float32, -lim, lim)
        gamma = jnp.ones((OUT_DIM,), jnp.float32)
        beta = jnp.zeros((OUT_DIM,), jnp.float32)
        return {'feature': feature, 'edge_index': edge_index, 'W': W, 'b': b, 'gamma': gamma, 'beta': beta}
    _L0_gnn_all = _L0_gnn_setup()
    _L0_gnn_in = {k: v for k, v in _L0_gnn_all.items() if k in ('W', 'b', 'gamma', 'beta')}
    del _L0_gnn_all

    def _L1_gnn_setup():
        import jax, jax.numpy as jnp
        import numpy as np
        N = 12500
        E = 200000
        F = 64
        H = 2
        C = 32
        NEG_SLOPE = 0.2

        def gat_layer(x, src, dst, Ws, Wd, a_s, a_d, b):
            n = x.shape[0]
            xs = (x @ Ws).reshape(n, H, C)
            xd = (x @ Wd).reshape(n, H, C)
            al_s = jnp.einsum('nhc,hc->nh', xs, a_s)
            al_d = jnp.einsum('nhc,hc->nh', xd, a_d)
            e = jax.nn.leaky_relu(al_s[src] + al_d[dst], negative_slope=NEG_SLOPE)
            m = jax.ops.segment_max(e, dst, num_segments=n)
            ex = jnp.exp(e - m[dst])
            den = jax.ops.segment_sum(ex, dst, num_segments=n)
            alpha = ex / den[dst]
            msg = xs[src] * alpha[:, :, None]
            out = jax.ops.segment_sum(msg, dst, num_segments=n)
            return out.reshape(n, H * C) + b
        key = jax.random.key(seed)
        ks = jax.random.split(key, 20)
        x = jax.random.normal(ks[0], (N, F), dtype=jnp.float32)
        edge_index = jax.random.randint(ks[1], (2, E), 0, N, dtype=jnp.int32)
        d = {'x': x, 'edge_index': edge_index}
        fan = {1: F, 2: H * C, 3: H * C}
        i = 2
        for l in (1, 2, 3):
            s = 1.0 / np.sqrt(fan[l])
            d[f'Ws{l}'] = jax.random.normal(ks[i], (fan[l], H * C), dtype=jnp.float32) * s
            i += 1
            d[f'Wd{l}'] = jax.random.normal(ks[i], (fan[l], H * C), dtype=jnp.float32) * s
            i += 1
            d[f'as{l}'] = jax.random.normal(ks[i], (H, C), dtype=jnp.float32) * (1.0 / np.sqrt(C))
            i += 1
            d[f'ad{l}'] = jax.random.normal(ks[i], (H, C), dtype=jnp.float32) * (1.0 / np.sqrt(C))
            i += 1
            d[f'b{l}'] = jnp.zeros((H * C,), dtype=jnp.float32)
        return d
    _L1_gnn_all = _L1_gnn_setup()
    _L1_gnn_in = {k: v for k, v in _L1_gnn_all.items() if k in ('Ws1', 'Wd1', 'as1', 'ad1', 'b1', 'Ws2', 'Wd2', 'as2', 'ad2', 'b2', 'Ws3', 'Wd3', 'as3', 'ad3', 'b3')}
    del _L1_gnn_all
    return {'x': x, 'src': src, 'dst': dst, 'L0_gnn_W': _L0_gnn_in['W'], 'L0_gnn_b': _L0_gnn_in['b'], 'L0_gnn_gamma': _L0_gnn_in['gamma'], 'L0_gnn_beta': _L0_gnn_in['beta'], 'L1_gnn_Ws1': _L1_gnn_in['Ws1'], 'L1_gnn_Wd1': _L1_gnn_in['Wd1'], 'L1_gnn_as1': _L1_gnn_in['as1'], 'L1_gnn_ad1': _L1_gnn_in['ad1'], 'L1_gnn_b1': _L1_gnn_in['b1'], 'L1_gnn_Ws2': _L1_gnn_in['Ws2'], 'L1_gnn_Wd2': _L1_gnn_in['Wd2'], 'L1_gnn_as2': _L1_gnn_in['as2'], 'L1_gnn_ad2': _L1_gnn_in['ad2'], 'L1_gnn_b2': _L1_gnn_in['b2'], 'L1_gnn_Ws3': _L1_gnn_in['Ws3'], 'L1_gnn_Wd3': _L1_gnn_in['Wd3'], 'L1_gnn_as3': _L1_gnn_in['as3'], 'L1_gnn_ad3': _L1_gnn_in['ad3'], 'L1_gnn_b3': _L1_gnn_in['b3']}

def reference(x, src, dst, L0_gnn_W, L0_gnn_b, L0_gnn_gamma, L0_gnn_beta, L1_gnn_Ws1, L1_gnn_Wd1, L1_gnn_as1, L1_gnn_ad1, L1_gnn_b1, L1_gnn_Ws2, L1_gnn_Wd2, L1_gnn_as2, L1_gnn_ad2, L1_gnn_b2, L1_gnn_Ws3, L1_gnn_Wd3, L1_gnn_as3, L1_gnn_ad3, L1_gnn_b3):
    import jax
    import jax.numpy as jnp

    def _L0_gnn_ref(feature, edge_index, W, b, gamma, beta):
        import jax, jax.numpy as jnp
        import numpy as np
        N_NODES = 12500
        N_EDGES = 200000
        IN_DIM = 64
        OUT_DIM = 64
        BN_EPS = 1e-05
        LRELU_SLOPE = 0.3
        src = edge_index[0]
        dst = edge_index[1]
        x_i = feature[dst]
        x_j = feature[src]
        h = jnp.concatenate([x_i, x_j - x_i], axis=-1)
        m = h @ W.T + b
        mu = jnp.mean(m, axis=0)
        var = jnp.var(m, axis=0)
        m = (m - mu) * jax.lax.rsqrt(var + BN_EPS) * gamma + beta
        m = jnp.where(m >= 0, m, LRELU_SLOPE * m)
        agg = jax.ops.segment_sum(m, dst, num_segments=N_NODES)
        cnt = jax.ops.segment_sum(jnp.ones((m.shape[0],), m.dtype), dst, num_segments=N_NODES)
        return agg / jnp.maximum(cnt, 1.0)[:, None]

    def _L1_gnn_ref(x, edge_index, Ws1, Wd1, as1, ad1, b1, Ws2, Wd2, as2, ad2, b2, Ws3, Wd3, as3, ad3, b3):
        import jax, jax.numpy as jnp
        import numpy as np
        N = 12500
        E = 200000
        F = 64
        H = 2
        C = 32
        NEG_SLOPE = 0.2

        def gat_layer(x, src, dst, Ws, Wd, a_s, a_d, b):
            n = x.shape[0]
            xs = (x @ Ws).reshape(n, H, C)
            xd = (x @ Wd).reshape(n, H, C)
            al_s = jnp.einsum('nhc,hc->nh', xs, a_s)
            al_d = jnp.einsum('nhc,hc->nh', xd, a_d)
            e = jax.nn.leaky_relu(al_s[src] + al_d[dst], negative_slope=NEG_SLOPE)
            m = jax.ops.segment_max(e, dst, num_segments=n)
            ex = jnp.exp(e - m[dst])
            den = jax.ops.segment_sum(ex, dst, num_segments=n)
            alpha = ex / den[dst]
            msg = xs[src] * alpha[:, :, None]
            out = jax.ops.segment_sum(msg, dst, num_segments=n)
            return out.reshape(n, H * C) + b
        src, dst = (edge_index[0], edge_index[1])
        h = jax.nn.relu(gat_layer(x, src, dst, Ws1, Wd1, as1, ad1, b1))
        h = jax.nn.relu(gat_layer(h, src, dst, Ws2, Wd2, as2, ad2, b2))
        h = gat_layer(h, src, dst, Ws3, Wd3, as3, ad3, b3)
        return h
    edge_index = jnp.stack([src, dst])
    x = _layernorm(x + _L0_gnn_ref(x, edge_index, L0_gnn_W, L0_gnn_b, L0_gnn_gamma, L0_gnn_beta), axis=-1)
    x = _layernorm(x + _L1_gnn_ref(x, edge_index, L1_gnn_Ws1, L1_gnn_Wd1, L1_gnn_as1, L1_gnn_ad1, L1_gnn_b1, L1_gnn_Ws2, L1_gnn_Wd2, L1_gnn_as2, L1_gnn_ad2, L1_gnn_b2, L1_gnn_Ws3, L1_gnn_Wd3, L1_gnn_as3, L1_gnn_ad3, L1_gnn_b3), axis=-1)
    return x

_drawn_inputs = setup_inputs


def setup_inputs(seed=0):
    import zlib

    import numpy as np

    out = dict(_drawn_inputs(seed))
    spreads = {'L0_gnn_gamma': (1.0, 0.2),
     'L0_gnn_beta': (0.0, 0.1),
     'L1_gnn_b1': (0.0, 0.1),
     'L1_gnn_b2': (0.0, 0.1),
     'L1_gnn_b3': (0.0, 0.1)}
    factors = {'L0_gnn_b': 64.0,
     'L1_gnn_Wd1': 64.0,
     'L1_gnn_ad1': 64.0,
     'L1_gnn_Wd2': 64.0,
     'L1_gnn_as2': 30.728,
     'L1_gnn_ad2': 64.0,
     'L1_gnn_Wd3': 64.0,
     'L1_gnn_as3': 64.0,
     'L1_gnn_ad3': 64.0}
    for name, (base, spread) in spreads.items():
        noise = np.random.default_rng([zlib.crc32(name.encode()), seed]).standard_normal(out[name].shape)
        drawn = base * np.exp(spread * noise) if base else spread * noise
        out[name] = jnp.asarray(drawn.astype(out[name].dtype))
    for name, factor in factors.items():
        out[name] = (out[name] * factor).astype(out[name].dtype)
    return out
```

```python
from contextlib import ExitStack

import numpy as np

import concourse.bass as bass
from concourse import mybir

P = 128
N, E, C, H, CH = 12500, 400000, 64, 2, 32
EPP = E // P
J = 25
SLOTS = 5
ITER = EPP // (J * SLOTS)
JI = J * SLOTS
CHUNKS = EPP // J
NPP = 98
NPAD = NPP * P
LASTN = N - (P - 1) * NPP
GN = 7
GROUPS = NPP // GN
PAIRS = GROUPS // 2
ROW = C + 4
SW = H * (CH + 1)
J1 = J + 1
QB = 33
LAYERS = 3
BIG = 3.0e38
BN_EPS, LN_EPS = 1e-5, 1e-5
SLOPE0, SLOPE1 = 0.3, 0.2
ONE_STEP = J * 16


def build(nc, x, src, dst, W0, b0, gamma, beta, Ws, Wd, a_s, a_d, bias, out):
    f32, i32 = mybir.dt.float32, mybir.dt.int32
    ALU, ACT, AX = mybir.AluOpType, mybir.ActivationFunctionType, mybir.AxisListType.X
    ctx = ExitStack()
    with ctx:
        def sb(name, shape, dt=f32):
            return ctx.enter_context(nc.sbuf_tensor(name, shape, dt))

        def ps(name, shape):
            return ctx.enter_context(nc.psum_tensor(name, shape, f32))

        def sem(name):
            return ctx.enter_context(nc.semaphore(name))

        def dram(name, shape, dt=f32):
            return nc.dram_tensor(name, shape, dt, kind="Internal").ap()

        table = dram("table", (NPAD, ROW))
        dst_term = dram("dst_term", (NPAD, C))
        sums = dram("sums", (E, ROW))
        conv_dst = dram("conv_dst", (E + NPAD, C))
        gat_dst = dram("gat_dst", (E + NPAD, 2))
        msgs = dram("msgs", (CHUNKS, P, C * J))
        samples = dram("samples", (P, EPP // J))

        src_ids = sb("src_ids", [P, EPP + JI], i32)
        keep = sb("keep", [P, EPP])
        reset = sb("reset", [P, EPP])
        feats = sb("feats", [P, NPP, C])
        rows = sb("rows", [P, SLOTS * J * ROW])
        ring_ids = sb("ring_ids", [P, JI], i32)
        X = sb("X", [P, SW * J1])
        F = sb("F", [P, SW * J1])
        S = sb("S", [P, SW * J1])
        stage_rows = sb("stage_rows", [P, J, ROW])
        ein = sb("ein", [P, C * J])
        z = sb("z", [P, C * J])
        z2 = sb("z2", [P, C * J])
        run_max = sb("run_max", [P, H, J1])
        logit0 = sb("logit0", [P, H, J])
        logit = sb("logit", [P, H, J])
        exps = sb("exps", [P, 2, H, J])
        alpha_raw = sb("alpha_raw", [P, JI, 2])
        alpha_e = sb("alpha_e", [P, H, JI + 1])
        node_rows = sb("node_rows", [P, 2, GN * ROW])
        hg = sb("hg", [P, GN, C])
        hg2 = sb("hg2", [P, GN, C])
        rden = sb("rden", [P, GN, H])
        mean = sb("mean", [P, GN])
        var = sb("var", [P, GN])
        hT = sb("hT", [C, GN * P])
        tstage = sb("tstage", [P, 2, GN * ROW])
        astage = sb("astage", [P, 2, GN * C])
        end_ids = sb("end_ids", [P, NPP + GN], i32)
        start_ids = sb("start_ids", [P, NPP], i32)
        end_ring = sb("end_ring", [P, 2, GN], i32)
        start_ring = sb("start_ring", [P, 2, GN], i32)
        has = sb("has", [P, NPP])
        first_ids = sb("first_ids", [P, 1], i32)
        patch_ids = sb("patch_ids", [P, 1], i32)
        first_rows = sb("first_rows", [P, ROW])
        ident = sb("ident", [P, P])
        ones = sb("ones", [P, P])
        w0 = sb("w0", [C, 2 * C])
        rhs0 = sb("rhs0", [C, 2 * C])
        ws = sb("ws", [C, LAYERS, C])
        wd = sb("wd", [C, LAYERS, C])
        asb = sb("asb", [C, LAYERS, C])
        adb = sb("adb", [C, LAYERS, C])
        wcat = sb("wcat", [C, LAYERS, ROW])
        wl = sb("wl", [C, ROW])
        biasb = sb("biasb", [P, LAYERS, C])
        b0b = sb("b0b", [P, C])
        gammab = sb("gammab", [P, C])
        betab = sb("betab", [P, C])
        stat = sb("stat", [P, 2, C])
        part = sb("part", [P, 2, C])
        bn = sb("bn", [P, 2, C])
        bn_s = sb("bn_s", [P, C])
        bn_t = sb("bn_t", [P, C])
        prev_i = sb("prev_i", [P, 1], i32)
        flags = sb("flags", [P, 6])
        edge0 = sb("edge0", [P, 1], i32)
        tmp_end, tmp_none, tmp_start = (sb(n, [P, NPP]) for n in ("tmp_end", "tmp_none", "tmp_start"))
        sq = sb("sq", [P, GN, C])
        bias_l = sb("bias_l", [P, C])
        first_row = sb("first_row", [P, P])
        query = sb("query", [P, NPP + 1])
        count = sb("count", [P, NPP + 1])
        qi = sb("qi", [P, NPP + 1], i32)
        blk = sb("blk", [P, QB])
        sub = sb("sub", [P, QB])
        blk_i = sb("blk_i", [P, QB], i32)
        sub_i = sb("sub_i", [P, QB], i32)
        reset_row = sb("reset_row", [SW, P])
        ends = sb("ends", [P, 2, SW])
        max_row = sb("max_row", [SW, P + 1])
        sum_row = sb("sum_row", [SW, P + 1])
        tail_row = sb("tail_row", [SW, 2, P])
        patch = sb("patch", [P, ROW])
        pmax = sb("pmax", [P, 3, SW])
        pexp = sb("pexp", [P, 2, SW])

        flat_feats = feats[:, :, :].rearrange("p n c -> p (n c)")
        dst_i = flat_feats[:, 0:EPP].bitcast(i32)
        D = flat_feats[:, EPP:2 * EPP]
        samp = ein[:, 0:EPP // J]
        cmp_b = rows[:, 0:QB * P].rearrange("p (q k) -> p q k", k=P)
        got2 = rows[:, QB * P:2 * QB * P].rearrange("p (q k) -> p q k", k=P)
        got3 = stage_rows[:, :, :].rearrange("p j r -> p (j r)")[:, 0:QB * J].bitcast(i32)\
            .rearrange("p (q k) -> p q k", k=J)
        got3f = stage_rows[:, :, :].rearrange("p j r -> p (j r)")[:, QB * J:2 * QB * J]\
            .rearrange("p (q k) -> p q k", k=J)

        slot_rows = rows[:, :].rearrange("p (s j r) -> p s j r", s=SLOTS, r=ROW)
        X4 = X[:, :].rearrange("p (h c j) -> p h c j", h=H, j=J1)
        F4 = F[:, :].rearrange("p (h c j) -> p h c j", h=H, j=J1)
        S3 = S[:, :].rearrange("p (c j) -> p c j", j=J1)
        X3 = X[:, :].rearrange("p (c j) -> p c j", j=J1)
        F3 = F[:, :].rearrange("p (c j) -> p c j", j=J1)
        z3 = z[:, :].rearrange("p (c j) -> p c j", j=J)
        z23 = z2[:, :].rearrange("p (c j) -> p c j", j=J)
        ein_jc = ein[:, :].rearrange("p (j c) -> p j c", c=C)
        node4 = [node_rows[:, k, :].rearrange("p (n r) -> p n r", r=ROW) for k in range(2)]
        tst = [tstage[:, k, :].rearrange("p (n r) -> p n r", r=ROW) for k in range(2)]
        ast = [astage[:, k, :].rearrange("p (n r) -> p n r", r=C) for k in range(2)]

        pT = ps("pT", [P, 2, 512])
        pP = ps("pP", [P, 512])
        pA = ps("pA", [P, 512])
        pR = ps("pR", [P, 512])
        pB = ps("pB", [P, 512])
        pS = ps("pS", [P, 512])

        in_dst, in_prev, in_src, in_x, in_w = (sem(n) for n in ("in_dst", "in_prev", "in_src", "in_x", "in_w"))
        zero_filled = sem("zero_filled")
        samples_in = sem("samples_in")
        searched2, searched3 = sem("searched2"), sem("searched3")
        table_written = [sem(f"table_written{k}") for k in range(2)]
        starts_scattered = [sem(f"starts_scattered{k}") for k in range(2)]
        firsts_gathered, firsts_written = sem("firsts_gathered"), sem("firsts_written")
        conv_gathered = [sem(f"conv_gathered{k}") for k in range(SLOTS)]
        gat_gathered = [sem(f"gat_gathered{k}") for k in range(SLOTS)]
        ein_loaded, msgs_stored, msgs_loaded, sums_stored = (
            sem(n) for n in ("ein_loaded", "msgs_stored", "msgs_loaded", "sums_stored"))
        alpha_loaded = sem("alpha_loaded")
        nodes_fetched = [sem(f"nodes_fetched{k}") for k in range(2)]
        patch_gathered, patch_scattered = sem("patch_gathered"), sem("patch_scattered")
        out_stored = sem("out_stored")
        zeros_ready, consts_ready, clears_done, dst_used = (
            sem(n) for n in ("zeros_ready", "consts_ready", "clears_done", "dst_used"))
        w0_T, w0_ready, wcat_ready = sem("w0_T"), sem("w0_ready"), sem("wcat_ready")
        dst_ready, firstrow_ready = sem("dst_ready"), sem("firstrow_ready")
        samples_ready = sem("samples_ready")
        search2_ready, search3_ready, ids_ready = sem("search2_ready"), sem("search3_ready"), sem("ids_ready")
        flag_ready, flag_T = sem("flag_ready"), sem("flag_T")
        pool_turn = sem("pool_turn")
        sp_turn, act_turn, pe_turn, dve_turn = (sem(n) for n in ("sp_turn", "act_turn", "pe_turn", "dve_turn"))
        h_ready, h_T, hT_ready, projected, staged = (
            sem(n) for n in ("h_ready", "h_T", "hT_ready", "projected", "staged"))
        stage_free = [sem(f"stage_free{k}") for k in range(2)]
        slot_ready = sem("slot_ready")
        ein_free, X_ready, X_free, z_ready, z_free = (
            sem(n) for n in ("ein_free", "X_ready", "X_free", "z_ready", "z_free"))
        stat_ready, stat_summed = sem("stat_ready"), sem("stat_summed")
        var_ready, dev_ready = sem("var_ready"), sem("dev_ready")
        bn_ready, scaled, shifted, conv_F, conv_free, conv_sum = (
            sem(n) for n in ("bn_ready", "scaled", "shifted", "conv_F", "conv_free", "conv_sum"))
        rows_staged, sums_free = sem("rows_staged"), sem("sums_free")
        alpha_free = sem("alpha_free")
        exps_in, weights_ready, gat_sum = sem("exps_in"), sem("weights_ready"), sem("gat_sum")
        node_ids = sem("node_ids")
        ends_ready, ends_T, tail_in, tail_exp, carry_ready, carry_T, patch_ready = (
            sem(n) for n in ("ends_ready", "ends_T", "tail_in", "tail_exp", "carry_ready", "carry_T", "patch_ready"))
        out_ready = sem("out_ready")

        x_p = x[0:(P - 1) * NPP, :].rearrange("(p i) c -> p i c", i=NPP)
        out_p = out[0:(P - 1) * NPP, :].rearrange("(p i) c -> p i c", i=NPP)
        PARTS = ((0, 112), (112, P - 1))
        table_p = table.rearrange("(p i) r -> p i r", i=NPP)
        dterm_p = dst_term.rearrange("(p i) r -> p i r", i=NPP)
        sums_p = sums.rearrange("(p j) r -> p j r", j=EPP)
        convd_p = conv_dst[0:E, :].rearrange("(p j) r -> p (j r)", j=EPP)
        gatd_p = gat_dst[0:E, :].rearrange("(p j) r -> p j r", j=EPP)
        dst_p = dst.rearrange("(p j) -> p j", j=EPP)
        dst_blocks = dst.rearrange("(b k) -> b k", k=J)

        block = ctx.enter_context(nc.Block())

        @block.sync
        def _(sp):
            def held(s, v):
                sp.wait_ge(s, v)
                sp.sem_inc(sp_turn, 1)

            sp.dma_start(dst_i, dst_p).then_inc(in_dst, 16)
            sp.wait_ge(clears_done, 1)
            with nc.allow_non_contiguous_dma(reason="one id per partition"):
                sp.dma_start(prev_i[1:P, :], dst_p[0:P - 1, EPP - 1:EPP]).then_inc(in_prev, 16)
            sp.dma_start(src_ids[:, 0:EPP], src.rearrange("(p j) -> p j", j=EPP)).then_inc(in_src, 16)
            sp.dma_start(src_ids[:, EPP:EPP + JI], src.rearrange("(p j) -> p j", j=EPP)[:, 0:JI]).then_inc(in_src, 16)
            sp.dma_start(w0[:, :], W0).then_inc(in_w, 16)
            for l in range(LAYERS):
                sp.dma_start(ws[:, l, :], Ws[l]).then_inc(in_w, 16)
                sp.dma_start(wd[:, l, :], Wd[l]).then_inc(in_w, 16)
                sp.dma_start(asb[:, l, :], a_s[l].rearrange("h c -> (h c)").partition_broadcast(C)).then_inc(in_w, 16)
                sp.dma_start(adb[:, l, :], a_d[l].rearrange("h c -> (h c)").partition_broadcast(C)).then_inc(in_w, 16)
                sp.dma_start(biasb[:, l, :], bias[l].partition_broadcast(P)).then_inc(in_w, 16)
            for t, v in ((b0b, b0), (gammab, gamma), (betab, beta)):
                sp.dma_start(t[:, :], v.partition_broadcast(P)).then_inc(in_w, 16)
            sp.wait_ge(samples_ready, 1)
            sp.dma_start(samples, samp).then_inc(samples_in, 16)
            sp.wait_ge(dst_used, 1)
            for lo, hi in PARTS:
                sp.dma_start(feats[lo:hi, :, :], x_p[lo:hi, :, :]).then_inc(in_x, 16)
            sp.dma_start(feats[P - 1:P, 0:LASTN, :], x[(P - 1) * NPP:N, :].rearrange("(a i) c -> a i c", a=1)).then_inc(in_x, 16)

            for k in range(2):
                sp.sem_inc(stage_free[k], 1)
            sp.sem_inc(z_free, 1)
            sp.sem_inc(sums_free, 1)
            sp.sem_inc(alpha_free, 1)

            def write_table(stage, h0):
                with sp.Fori(0, PAIRS) as it:
                    for k in range(2):
                        held(staged, 2 * (h0 + it) + k + 2)
                        sp.dma_start(table_p[:, bass.ds((2 * it + k) * GN, GN), :], tst[k]).then_inc(table_written[k], 16)
                        if stage == 0:
                            sp.dma_start(dterm_p[:, bass.ds((2 * it + k) * GN, GN), :], ast[k]).then_inc(table_written[k], 16)
                    for k in range(2):
                        done = h0 + it + 1
                        held(table_written[k], 32 * (it + 1) if stage == 0 else 16 * (done + PAIRS))
                        held(starts_scattered[k], 16 * GN * done)
                        sp.sem_inc(stage_free[k], 1)

            write_table(0, 0)
            sp.wait_ge(firsts_gathered, 16)
            sp.dma_start(convd_p[:, 0:C], first_rows[:, 0:C]).then_inc(firsts_written, 16)
            sp.wait_ge(firsts_written, 16)

            with sp.Fori(0, CHUNKS) as c:
                held(ein_free, c + 1)
                sp.dma_start(ein[:, :], convd_p[:, bass.ds(c * (J * C), J * C)]).then_inc(ein_loaded, 16)
                held(z_ready, c + 1)
                sp.dma_start(msgs[bass.ds(c, 1), :, :].rearrange("a p n -> (a p) n"), z[:, :]).then_inc(msgs_stored, 16)
                held(msgs_stored, 16 * (c + 1))
                sp.sem_inc(z_free, 1)

            def store_sums(base, c, row0):
                held(rows_staged, base + c + 1)
                sp.dma_start(sums_p[:, bass.ds(row0, J), :], stage_rows[:, :, :]).then_inc(sums_stored, 16)
                held(sums_stored, 16 * (base + c + 1))
                sp.sem_inc(sums_free, 1)

            with sp.Fori(0, CHUNKS) as c:
                held(scaled, c + 1)
                sp.dma_start(ein[:, :], msgs[bass.ds(c, 1), :, :].rearrange("a p n -> (a p) n")).then_inc(msgs_loaded, 16)
                store_sums(0, c, c * J)

            def gat_layer(L):
                write_table(1, (L + 1) * PAIRS)
                held(firsts_gathered, 16 * (L + 2))
                with nc.allow_non_contiguous_dma(reason="two values per partition"):
                    sp.dma_start(gatd_p[:, 0:1, :].rearrange("p a r -> p (a r)"), first_rows[:, C + 2:ROW]).then_inc(firsts_written, 16)
                held(firsts_written, 16 * (L + 2))
                with sp.Fori(0, ITER) as it:
                    held(alpha_free, L * ITER + it + 1)
                    sp.dma_start(alpha_raw[:, :, :], gatd_p[:, bass.ds(it * JI, JI), :]).then_inc(alpha_loaded, 16)
                    for b in range(SLOTS):
                        store_sums((L + 1) * CHUNKS, it * SLOTS + b, it * JI + b * J)

            with sp.Fori(0, LAYERS) as L:
                gat_layer(L)

            sp.wait_ge(out_ready, GROUPS)
            for lo, hi in PARTS:
                sp.dma_start(out_p[lo:hi, :, :], feats[lo:hi, :, :]).then_inc(out_stored, 16)
            sp.dma_start(out[(P - 1) * NPP:N, :].rearrange("(a i) c -> a i c", a=1), feats[P - 1:P, 0:LASTN, :]).then_inc(out_stored, 16)
            sp.wait_ge(out_stored, 48)

        @block.gpsimd
        def _(pool):
            def at(col):
                return bass.IndirectOffsetOnAxis(ap=col, axis=0)

            def gather(out_, table_, col):
                return pool.indirect_dma_start(out=out_, out_offset=None, in_=table_, in_offset=at(col))

            def scatter(table_, col, in_):
                return pool.indirect_dma_start(out=table_, out_offset=at(col), in_=in_, in_offset=None)

            pool.memset(ident[:, :], 0.0)
            pool.iota(qi[:, :], pattern=[[1, NPP + 1]], base=-1, channel_multiplier=NPP)
            pool.iota(edge0[:, :], pattern=[[1, 1]], base=0, channel_multiplier=EPP)
            pool.drain()
            pool.affine_select(out=ident[:, :], in_=ident[:, :], compare_op=ALU.not_equal, fill=1.0, base=0,
                               pattern=[[-1, P]], channel_multiplier=1).then_inc(consts_ready, 1)

            pool.wait_ge(samples_in, 16)
            with pool.Fori(0, 3) as it:
                pool.wait_ge(search2_ready, it + 1)
                pool.sem_inc(pool_turn, 1)
                for q in range(QB):
                    gather(got2[:, q, 0:EPP // J], samples, blk_i[:, q:q + 1]).then_inc(searched2, 16)
                pool.wait_ge(search3_ready, it + 1)
                pool.sem_inc(pool_turn, 1)
                for q in range(QB):
                    gather(got3[:, q, :], dst_blocks, sub_i[:, q:q + 1]).then_inc(searched3, 16)

            def scatter_starts(k, target, values):
                for n in range(GN):
                    scatter(target, start_ring[:, k, n:n + 1], values[:, n, :]).then_inc(starts_scattered[k], 16)

            def gather_firsts(source, width, uses):
                for k in range(2):
                    pool.wait_ge(stage_free[k], uses + 1)
                pool.sem_inc(pool_turn, 1)
                gather(first_rows[:, 0:width], source, first_ids[:, 0:1]).then_inc(firsts_gathered, 16)

            def edge_gathers(gathered, K0):
                with pool.Fori(0, ITER) as it:
                    for b in range(SLOTS):
                        pool.wait_ge(slot_ready, K0 + it * SLOTS + b + 1)
                        pool.sem_inc(pool_turn, 1)
                        for j in range(J):
                            gather(slot_rows[:, b, j, :], table, ring_ids[:, b * J + j:b * J + j + 1])\
                                .then_inc(gathered[b], 16)

            def complete_first_rows(t):
                pool.wait_ge(sums_free, (t + 1) * CHUNKS + 1)
                pool.sem_inc(pool_turn, 1)
                gather(patch[:, :], sums, patch_ids[:, 0:1]).then_inc(patch_gathered, 16)
                pool.wait_ge(patch_ready, t + 1)
                pool.sem_inc(pool_turn, 1)
                scatter(sums, patch_ids[:, 0:1], patch[:, :]).then_inc(patch_scattered, 16)
                pool.wait_ge(patch_scattered, 16 * (t + 1))
                pool.sem_inc(pool_turn, 1)

            def fetch_nodes(t, it, k):
                pool.wait_ge(node_ids, t * (GROUPS + 1) + 2 * it + k + 1)
                pool.sem_inc(pool_turn, 1)
                for n in range(GN):
                    gather(node4[k][:, n, :], sums, end_ring[:, k, n:n + 1]).then_inc(nodes_fetched[k], 16)

            pool.wait_ge(zero_filled, 16 * (ITER + 1))
            with pool.Fori(0, PAIRS) as it:
                for k in range(2):
                    pool.wait_ge(staged, 2 * it + k + 2)
                    pool.sem_inc(pool_turn, 1)
                    scatter_starts(k, conv_dst, ast[k])
            gather_firsts(dst_term, C, PAIRS)
            edge_gathers(conv_gathered, 0)

            with pool.Fori(0, CHUNKS) as c:
                pool.wait_ge(msgs_loaded, 16 * (c + 1))
                pool.sem_inc(pool_turn, 1)
                pool.wait_ge(shifted, c + 1)
                pool.tensor_tensor(z3, ein[:, :].rearrange("p (c j) -> p c j", j=J),
                                   bn_s[:, :, None].to_broadcast([P, C, J]), ALU.mult).then_inc(scaled, 1)

            with pool.Fori(0, LAYERS) as L:
                complete_first_rows(L)
                with pool.Fori(0, PAIRS) as it:
                    for k in range(2):
                        fetch_nodes(L, it, k)
                    for k in range(2):
                        pool.wait_ge(staged, (L + 1) * GROUPS + 2 * it + k + 2)
                        pool.sem_inc(pool_turn, 1)
                        scatter_starts(k, gat_dst, tst[k][:, :, C + 2:ROW])
                gather_firsts(table, ROW, (L + 2) * PAIRS)
                edge_gathers(gat_gathered, (L + 1) * CHUNKS)
            complete_first_rows(LAYERS)
            with pool.Fori(0, PAIRS) as it:
                for k in range(2):
                    fetch_nodes(LAYERS, it, k)

        @block.scalar
        def _(act):
            def held(s, v):
                act.wait_ge(s, v)
                act.sem_inc(act_turn, 1)

            act.wait_ge(zeros_ready, 1)
            with act.Fori(0, ITER) as it:
                act.dma_start(convd_p[:, bass.ds(it * (JI * C), JI * C)].rearrange("p (a n) -> p a n", a=SLOTS),
                              z[:, None, :].to_broadcast([P, SLOTS, J * C])).then_inc(zero_filled, 16)
            act.dma_start(gatd_p[:, :, :].rearrange("p (a j) r -> p a (j r)", a=5),
                          z[:, None, 0:EPP * 2 // 5].to_broadcast([P, 5, EPP * 2 // 5])).then_inc(zero_filled, 16)
            act.sem_inc(staged, 1)
            act.sem_inc(ein_free, 1)
            act.wait_ge(ids_ready, 1)

            def project(stage, h0):
                with act.Fori(0, PAIRS) as it:
                    for k in range(2):
                        q = 2 * (h0 + it) + k
                        if stage == 1:
                            deviation(2 * it + k)
                        act.wait_ge(h_T, q + 2)
                        nc.scalar.copy(hT[:, 0:4 * P], pT[0:C, 0, 0:4 * P])
                        nc.scalar.copy(hT[:, 4 * P:GN * P], pT[0:C, 1, 0:3 * P]).then_inc(hT_ready, 1)
                        act.wait_ge(projected, q + 1)
                        act.sem_inc(act_turn, 1)
                        held(stage_free[k], h0 + it + 1)
                        nc.scalar.copy(start_ring[:, k, :], start_ids[:, bass.ds((2 * it + k) * GN, GN)])
                        if stage == 0:
                            nc.scalar.copy(ast[k], pA[:, 0:GN * C].rearrange("p (n r) -> p n r", r=C))
                        nc.scalar.copy(tst[k], pP[:, 0:GN * ROW].rearrange("p (n r) -> p n r", r=ROW)).then_inc(staged, 1)

            def deviation(i):
                act.wait_ge(var_ready, i + 1)
                nc.scalar.activation(var[:, :], var[:, :], ACT.Sqrt).then_inc(dev_ready, 1)

            def tails(t):
                act.wait_ge(tail_in, 2 * t + 1)
                nc.scalar.activation(tail_row[:, :, :], tail_row[:, :, :], ACT.Exp).then_inc(tail_exp, 1)
                act.wait_ge(tail_in, 2 * t + 2)
                nc.scalar.activation(pexp[:, :, :], pexp[:, :, :], ACT.Exp).then_inc(tail_exp, 1)

            project(0, 0)
            with act.Fori(0, CHUNKS) as c:
                act.wait_ge(ein_loaded, 16 * (c + 1))
                act.sem_inc(act_turn, 1)
                held(X_free, c + 1)
                nc.scalar.copy(F3[:, 0:C, 1:J1], keep[:, None, bass.ds(c * J, J)].to_broadcast([P, C, J]))
                nc.scalar.copy(X3[:, 0:C, 1:J1], ein_jc.rearrange("p j c -> p c j")).then_inc(X_ready, 1)
                act.drain().then_inc(ein_free, 1)

            act.wait_ge(bn_ready, 1)
            nc.scalar.activation(part[:, 0, :], part[:, 0, :], ACT.Sqrt).then_inc(dev_ready, 1)
            with act.Fori(0, CHUNKS) as c:
                held(conv_free, c + 1)
                nc.scalar.copy(F3[:, :, 1:J1], keep[:, None, bass.ds(c * J, J)].to_broadcast([P, SW, J])).then_inc(conv_F, 1)
                act.wait_ge(conv_sum, c + 1)
                act.sem_inc(act_turn, 1)
                act.wait_ge(sums_free, c + 1)
                nc.scalar.copy(stage_rows[:, :, 0:SW], S3[:, :, 1:J1].rearrange("p c j -> p j c")).then_inc(rows_staged, 1)

            def gat_pass(L):
                with act.Fori(0, ITER) as it:
                    for b in range(SLOTS):
                        K = L * CHUNKS + it * SLOTS + b
                        act.wait_ge(exps_in, K + 1)
                        for h in range(H):
                            nc.scalar.activation(F4[:, h, :, 1:J1],
                                                 exps[:, 0, h, None, :].to_broadcast([P, CH + 1, J]), ACT.Exp)
                        nc.scalar.activation(X4[:, :, CH, 1:J1], exps[:, 1, :, :], ACT.Exp).then_inc(weights_ready, 1)
                        act.wait_ge(gat_sum, K + 1)
                        act.sem_inc(act_turn, 1)
                        act.wait_ge(sums_free, CHUNKS + K + 1)
                        nc.scalar.copy(stage_rows[:, :, SW:ROW], run_max[:, :, 1:J1].rearrange("p h j -> p j h"))
                        nc.scalar.copy(stage_rows[:, :, 0:SW], S3[:, :, 1:J1].rearrange("p c j -> p j c")).then_inc(rows_staged, 1)
            tails(0)
            project(1, PAIRS)
            gat_pass(0)
            with act.Fori(1, LAYERS) as L:
                tails(L)
                project(2, (L + 1) * PAIRS)
                gat_pass(L)
            tails(LAYERS)
            with act.Fori(0, GROUPS) as g:
                deviation(GROUPS + g)

        @block.tensor
        def _(pe):
            pe.wait_ge(in_w, 16 * (1 + 5 * LAYERS + 3))
            pe.wait_ge(consts_ready, 1)
            for k in range(2):
                last = nc.tensor.transpose(pT[0:C, 0, k * C:(k + 1) * C], w0[:, k * C:(k + 1) * C], ident[0:C, 0:C])
            last.then_inc(w0_T, 1)
            pe.wait_ge(dst_ready, 1)
            nc.tensor.matmul(pR[:, 0:P], first_row[:, :], ident[:, :], start=True, stop=True).then_inc(firstrow_ready, 1)
            pe.wait_ge(flag_ready, 1)
            nc.tensor.transpose(pR[0:SW, 0:P], ends[:, 0, :], ident[:, :]).then_inc(flag_T, 1)
            pe.sem_inc(h_T, 1)
            pe.wait_ge(w0_ready, 1)

            def project(stage, h0):
                with pe.Fori(0, PAIRS) as it:
                    for k in range(2):
                        q = 2 * (h0 + it) + k
                        pe.wait_ge(h_ready, q + 1)
                        pe.sem_inc(pe_turn, 1)
                        for n in range(GN):
                            last = nc.tensor.transpose(pT[0:C, n // 4, (n % 4) * P:(n % 4 + 1) * P], hg[:, n, :], ident[:, :])
                        last.then_inc(h_T, 1)
                        pe.wait_ge(staged, q + 1)
                        pe.sem_inc(pe_turn, 1)
                        pe.wait_ge(hT_ready, q + 1)
                        for n in range(GN):
                            lhsT = hT[:, n * P:(n + 1) * P]
                            if stage == 0:
                                nc.tensor.matmul(pA[:, n * C:(n + 1) * C], lhsT, rhs0[:, C:2 * C], start=True, stop=True)
                            last = nc.tensor.matmul(pP[:, n * ROW:(n + 1) * ROW], lhsT, wl[:, :], start=True, stop=True)
                        last.then_inc(projected, 1)

            def tails(t):
                pe.wait_ge(ends_ready, t + 1)
                pe.sem_inc(pe_turn, 1)
                for k in range(2):
                    last = nc.tensor.transpose(pR[0:SW, k * P:(k + 1) * P], ends[:, k, :], ident[:, :])
                last.then_inc(ends_T, 1)
                pe.wait_ge(carry_ready, t + 1)
                pe.sem_inc(pe_turn, 1)
                nc.tensor.transpose(pB[:, 0:SW], sum_row[:, 0:P], ident[0:SW, 0:SW])
                nc.tensor.transpose(pB[:, P:P + SW], max_row[:, 0:P], ident[0:SW, 0:SW]).then_inc(carry_T, 1)

            project(0, 0)
            pe.wait_ge(stat_ready, 1)
            nc.tensor.matmul(pS[:, 0:2 * C], ones[:, :], stat[:, :, :].rearrange("p a c -> p (a c)"),
                             start=True, stop=True).then_inc(stat_summed, 1)
            with pe.Fori(0, LAYERS) as L:
                tails(L)
                project(1, (L + 1) * PAIRS)
            tails(LAYERS)

        @block.vector
        def _(dve):
            v = nc.vector

            def bc(ap, shape):
                return ap.to_broadcast(shape)

            v.memset(z[:, :], 0.0).then_inc(zeros_ready, 1)
            v.memset(prev_i[:, :], -1)
            dve.drain().then_inc(clears_done, 1)
            v.memset(ones[:, :], 1.0)
            for buf in (run_max[:, :, :], alpha_e[:, :, :], max_row[:, :], sum_row[:, :], stat[:, :, :], rhs0[:, :],
                        wcat[:, :, :], end_ids[:, :], z2[:, :], first_row[:, :]):
                v.memset(buf, 0.0)

            dve.wait_ge(in_dst, 16)
            v.tensor_copy(D, dst_i)
            dve.drain()
            v.tensor_copy(samp, D[:, 0:EPP:J]).then_inc(samples_ready, 1)
            v.tensor_copy(first_row[:, :], bc(D[:, 0:1], [P, P])).then_inc(dst_ready, 1)
            v.tensor_copy(first_ids[:, :], D[:, 0:1])
            v.tensor_tensor(keep[:, 1:EPP], D[:, 1:EPP], D[:, 0:EPP - 1], ALU.is_equal)
            v.memset(keep[:, 0:1], 0.0)
            v.tensor_scalar(reset[:, :], D, D[:, 0:1], None, ALU.is_equal)
            v.tensor_tensor(flags[:, 1:2], D[:, 0:1], D[:, EPP - 1:EPP], ALU.is_equal)
            dve.wait_ge(in_prev, 16)
            v.tensor_copy(flags[:, 4:5], prev_i[:, :])
            dve.wait_ge(consts_ready, 1)
            v.tensor_copy(query[:, :], qi[:, :])
            dve.drain()
            v.tensor_tensor(flags[:, 0:1], D[:, 0:1], flags[:, 4:5], ALU.is_equal)
            v.tensor_reduce(flags[:, 2:3], reset[:, :], AX, ALU.add)
            dve.drain()
            v.tensor_tensor(flags[:, 3:4], flags[:, 0:1], flags[:, 1:2], ALU.mult)
            v.tensor_scalar(reset[:, :], keep[:, :], BIG, BIG, ALU.mult, ALU.subtract)
            v.tensor_copy(flags[:, 5:6], edge0[:, :])
            v.memset(feats[96:P, LASTN:NPP, :], 0.0).then_inc(dst_used, 1)
            dve.drain()
            v.scalar_tensor_tensor(flags[:, 4:5], flags[:, 2:3], -1.0, flags[:, 5:6], ALU.add, ALU.add)
            v.tensor_scalar(flags[:, 3:4], flags[:, 3:4], BIG, BIG, ALU.mult, ALU.subtract)
            v.tensor_scalar(flags[:, 0:1], flags[:, 0:1], BIG, BIG, ALU.mult, ALU.subtract)
            dve.drain()
            v.tensor_copy(patch_ids[:, :], flags[:, 4:5])

            dve.wait_ge(firstrow_ready, 1)
            v.tensor_copy(first_row[:, :], pR[:, 0:P])
            dve.drain()
            v.tensor_copy(ends[:, 0, :], bc(flags[:, 3:4], [P, SW])).then_inc(flag_ready, 1)
            with dve.Fori(0, 3) as it:
                mine = query[:, bass.ds(it * QB, QB)]
                v.tensor_tensor(cmp_b, mine[:, :, None].to_broadcast([P, QB, P]),
                                first_row[:, None, :].to_broadcast([P, QB, P]), ALU.is_ge)
                dve.drain()
                v.tensor_reduce(blk[:, :], cmp_b, AX, ALU.add)
                dve.drain()
                v.tensor_scalar(blk[:, :], blk[:, :], -1.0, 0.0, ALU.add, ALU.max)
                dve.drain()
                v.tensor_copy(blk_i[:, :], blk[:, :]).then_inc(search2_ready, 1)
                dve.wait_ge(searched2, 16 * QB * (it + 1))
                v.tensor_tensor(cmp_b[:, :, 0:EPP // J], mine[:, :, None].to_broadcast([P, QB, EPP // J]),
                                got2[:, :, 0:EPP // J], ALU.is_ge)
                dve.drain()
                v.tensor_reduce(sub[:, :], cmp_b[:, :, 0:EPP // J], AX, ALU.add)
                dve.drain()
                v.tensor_scalar(sub[:, :], sub[:, :], -1.0, 0.0, ALU.add, ALU.max)
                dve.drain()
                v.scalar_tensor_tensor(sub[:, :], blk[:, :], float(EPP // J), sub[:, :], ALU.mult, ALU.add)
                dve.drain()
                v.tensor_copy(sub_i[:, :], sub[:, :]).then_inc(search3_ready, 1)
                dve.wait_ge(searched3, 16 * QB * (it + 1))
                v.tensor_copy(got3f, got3)
                dve.drain()
                v.tensor_tensor(cmp_b[:, :, 0:J], mine[:, :, None].to_broadcast([P, QB, J]), got3f, ALU.is_ge)
                dve.drain()
                v.tensor_reduce(blk[:, :], cmp_b[:, :, 0:J], AX, ALU.add)
                dve.drain()
                v.scalar_tensor_tensor(count[:, bass.ds(it * QB, QB)], sub[:, :], float(J), blk[:, :], ALU.mult, ALU.add)
                dve.drain()
            v.tensor_tensor(has[:, :], count[:, 1:NPP + 1], count[:, 0:NPP], ALU.is_gt)
            v.tensor_scalar(tmp_end[:, :], count[:, 1:NPP + 1], -1.0, 0.0, ALU.add, ALU.max)
            v.tensor_scalar(tmp_none[:, :], query[:, 1:NPP + 1], float(E), None, ALU.add)
            dve.drain()
            v.tensor_copy(end_ids[:, 0:NPP], tmp_end[:, :])
            v.tensor_tensor(tmp_start[:, :], count[:, 0:NPP], tmp_none[:, :], ALU.subtract)
            dve.drain()
            v.tensor_tensor(tmp_start[:, :], tmp_start[:, :], has[:, :], ALU.mult)
            dve.drain()
            v.tensor_tensor(tmp_start[:, :], tmp_start[:, :], tmp_none[:, :], ALU.add)
            dve.drain()
            dve.wait_ge(in_src, 32)
            v.tensor_copy(ring_ids[:, :], src_ids[:, 0:JI])
            v.tensor_copy(start_ids[:, :], tmp_start[:, :]).then_inc(ids_ready, 1)

            dve.wait_ge(flag_T, 1)
            v.tensor_copy(reset_row[:, :], pR[0:SW, 0:P])
            dve.wait_ge(w0_T, 1)
            v.tensor_copy(rhs0[:, 0:C], pT[0:C, 0, C:2 * C])
            v.tensor_copy(wl[:, 0:C], pT[0:C, 0, C:2 * C])
            v.memset(wl[:, C:ROW], 0.0)
            dve.drain()
            v.tensor_tensor(rhs0[:, C:2 * C], pT[0:C, 0, 0:C], rhs0[:, 0:C], ALU.subtract).then_inc(w0_ready, 1)
            dve.wait_ge(in_w, 16 * (1 + 5 * LAYERS + 3))
            v.tensor_tensor(asb[:, :, :], ws[:, :, :], asb[:, :, :], ALU.mult)
            v.tensor_tensor(adb[:, :, :], wd[:, :, :], adb[:, :, :], ALU.mult)
            v.tensor_copy(wcat[:, :, 0:C], ws[:, :, :])
            dve.drain()
            v.tensor_reduce(wcat[:, :, C:C + 2], asb[:, :, :].rearrange("k l (h c) -> k l h c", h=H), AX, ALU.add)
            v.tensor_reduce(wcat[:, :, C + 2:ROW], adb[:, :, :].rearrange("k l (h c) -> k l h c", h=H), AX, ALU.add)

            for buf in (X, F, S):
                v.memset(buf[:, :], 0.0)
            v.memset(stage_rows[:, :, :], 0.0)
            dve.drain().then_inc(X_free, 1)
            dve.sem_inc(slot_ready, SLOTS)
            dve.sem_inc(shifted, 1)

            dve.wait_ge(in_x, 48)
            dve.sem_inc(dve_turn, 1)
            with dve.Fori(0, PAIRS) as it:
                for k in range(2):
                    dve.wait_ge(h_T, 2 * it + k + 1)
                    dve.sem_inc(dve_turn, 1)
                    v.tensor_copy(hg[:, :, :], feats[:, bass.ds((2 * it + k) * GN, GN), :]).then_inc(h_ready, 1)

            with dve.Fori(0, ITER) as it:
                for b in range(SLOTS):
                    c = it * SLOTS + b
                    dve.wait_ge(X_ready, c + 1)
                    v.tensor_copy(X3[:, 0:C, 0:1], S3[:, 0:C, J:J1])
                    dve.drain()
                    v.tensor_tensor_scan(S[:, 0:C * J1], F[:, 0:C * J1], X[:, 0:C * J1], 0.0, ALU.mult, ALU.add)\
                        .then_inc(X_free, 1)
                    dve.drain()
                    dve.wait_ge(conv_gathered[b], ONE_STEP * (it + 1))
                    dve.sem_inc(dve_turn, 1)
                    dve.wait_ge(z_free, c + 1)
                    v.tensor_tensor(z3, S3[:, 0:C, 1:J1], slot_rows[:, b, :, 0:C].rearrange("p j c -> p c j"),
                                    ALU.add).then_inc(z_ready, 1)
                    dve.drain()
                    v.tensor_copy(ring_ids[:, b * J:(b + 1) * J], src_ids[:, bass.ds((it + 1) * JI + b * J, J)])\
                        .then_inc(slot_ready, 1)
                    v.tensor_tensor(z2[:, :], z[:, :], z[:, :], ALU.mult)
                    v.tensor_reduce(part[:, 0, :], z3, AX, ALU.add)
                    dve.drain()
                    v.tensor_reduce(part[:, 1, :], z23, AX, ALU.add)
                    dve.drain()
                    v.tensor_tensor(stat[:, :, :], stat[:, :, :], part[:, :, :], ALU.add)
            dve.drain().then_inc(stat_ready, 1)

            dve.wait_ge(stat_summed, 1)
            v.tensor_scalar(bn[:, :, :].rearrange("p a c -> p (a c)"), pS[:, 0:2 * C], 1.0 / E, None, ALU.mult)
            dve.drain()
            v.tensor_tensor(part[:, 0, :], bn[:, 0, :], bn[:, 0, :], ALU.mult)
            v.tensor_tensor(part[:, 1, :], bn[:, 0, :], b0b[:, :], ALU.add)
            dve.drain()
            v.tensor_tensor(part[:, 0, :], bn[:, 1, :], part[:, 0, :], ALU.subtract)
            v.tensor_tensor(part[:, 1, :], b0b[:, :], part[:, 1, :], ALU.subtract)
            dve.drain()
            v.tensor_scalar(part[:, 0, :], part[:, 0, :], 0.0, BN_EPS, ALU.max, ALU.add)
            dve.drain().then_inc(bn_ready, 1)
            dve.wait_ge(dev_ready, 1)
            v.reciprocal(part[:, 0, :], part[:, 0, :])
            dve.drain()
            v.tensor_tensor(bn_s[:, :], part[:, 0, :], gammab[:, :], ALU.mult)
            dve.drain()
            v.tensor_tensor(part[:, 1, :], part[:, 1, :], bn_s[:, :], ALU.mult)
            dve.drain()
            v.tensor_tensor(bn_t[:, :], part[:, 1, :], betab[:, :], ALU.add)
            v.memset(X4[:, :, CH, 1:J1], 1.0)
            dve.drain().then_inc(scaled, 1)
            dve.sem_inc(conv_free, 1)

            with dve.Fori(0, CHUNKS) as c:
                dve.wait_ge(scaled, c + 2)
                v.tensor_tensor(z23, z3, bn_t[:, :, None].to_broadcast([P, C, J]), ALU.add).then_inc(shifted, 1)
                v.tensor_copy(X3[:, :, 0:1], S3[:, :, J:J1])
                dve.drain()
                for h in range(H):
                    zh = z23[:, h * CH:(h + 1) * CH, :]
                    v.scalar_tensor_tensor(X4[:, h, 0:CH, 1:J1], zh, SLOPE0, zh, ALU.mult, ALU.max)
                dve.drain()
                dve.wait_ge(conv_F, c + 1)
                v.tensor_tensor_scan(S[:, :], F[:, :], X[:, :], 0.0, ALU.mult, ALU.add).then_inc(conv_sum, 1)
                dve.drain().then_inc(conv_free, 1)
                dve.wait_ge(rows_staged, c + 1)
                dve.sem_inc(dve_turn, 1)

            def complete_first_rows(t):
                last_row = stage_rows[:, J - 1, :]
                v.tensor_copy(ends[:, 0, :], last_row[:, 0:SW])
                for h in range(H):
                    last = v.tensor_copy(ends[:, 1, h * (CH + 1):(h + 1) * (CH + 1)],
                                         bc(last_row[:, SW + h:SW + h + 1], [P, CH + 1]))
                last.then_inc(ends_ready, 1)
                dve.wait_ge(ends_T, t + 1)
                v.tensor_tensor_scan(max_row[:, 1:P + 1], reset_row[:, :], pR[0:SW, P:2 * P], 0.0, ALU.add, ALU.max)
                dve.drain()
                v.tensor_tensor(tail_row[:, 0, :], max_row[:, 0:P], reset_row[:, :], ALU.add)
                v.tensor_tensor(tail_row[:, 1, :], pR[0:SW, P:2 * P], max_row[:, 1:P + 1], ALU.subtract)
                dve.drain()
                v.tensor_tensor(tail_row[:, 0, :], tail_row[:, 0, :], max_row[:, 1:P + 1], ALU.subtract).then_inc(tail_in, 1)
                dve.wait_ge(tail_exp, 2 * t + 1)
                v.tensor_tensor(tail_row[:, 1, :], tail_row[:, 1, :], pR[0:SW, 0:P], ALU.mult)
                dve.drain()
                v.tensor_tensor_scan(sum_row[:, 1:P + 1], tail_row[:, 0, :], tail_row[:, 1, :], 0.0, ALU.mult, ALU.add)\
                    .then_inc(carry_ready, 1)
                dve.wait_ge(patch_gathered, 16 * (t + 1))
                for h in range(H):
                    v.tensor_copy(pmax[:, 0, h * (CH + 1):(h + 1) * (CH + 1)],
                                  bc(patch[:, SW + h:SW + h + 1], [P, CH + 1]))
                dve.wait_ge(carry_T, t + 1)
                v.tensor_scalar(pmax[:, 1, :], pB[:, P:P + SW], flags[:, 0:1], None, ALU.add)
                dve.drain()
                v.tensor_tensor(pmax[:, 2, :], pmax[:, 0, :], pmax[:, 1, :], ALU.max)
                dve.drain()
                v.tensor_tensor(pexp[:, 0, :], pmax[:, 0, :], pmax[:, 2, :], ALU.subtract)
                v.tensor_tensor(pexp[:, 1, :], pmax[:, 1, :], pmax[:, 2, :], ALU.subtract).then_inc(tail_in, 1)
                dve.wait_ge(tail_exp, 2 * t + 2)
                v.tensor_tensor(pexp[:, 0, :], pexp[:, 0, :], patch[:, 0:SW], ALU.mult)
                v.tensor_tensor(pexp[:, 1, :], pexp[:, 1, :], pB[:, 0:SW], ALU.mult)
                dve.drain()
                v.tensor_tensor(patch[:, 0:SW], pexp[:, 0, :], pexp[:, 1, :], ALU.add).then_inc(patch_ready, 1)

            def put_ids(g, k):
                v.tensor_copy(end_ring[:, k, :], end_ids[:, bass.ds(g * GN, GN)]).then_inc(node_ids, 1)

            def node_means(t, it, k, q):
                g = 2 * it + k
                dve.drain()
                put_ids(g + 1, 1 - k)
                dve.wait_ge(nodes_fetched[k], 16 * GN * (t * PAIRS + it + 1))
                r = node4[k][:, :, 0:SW].rearrange("p n (h c) -> p n h c", h=H)
                v.reciprocal(rden[:, :, :], r[:, :, :, CH])
                dve.drain()
                v.tensor_tensor(rden[:, :, :], rden[:, :, :],
                                has[:, bass.ds(g * GN, GN)][:, :, None].to_broadcast([P, GN, H]), ALU.mult)
                dve.drain()
                if q is not None:
                    dve.wait_ge(h_T, q + 1)
                    dve.sem_inc(dve_turn, 1)
                v.tensor_tensor(hg2[:, :, :].rearrange("p n (h c) -> p n h c", h=H), r[:, :, :, 0:CH],
                                rden[:, :, :, None].to_broadcast([P, GN, H, CH]), ALU.mult)
                dve.drain()

            def layer_norm(g, i, target):
                mine = feats[:, bass.ds(g * GN, GN), :]
                v.tensor_tensor(hg2[:, :, :], hg2[:, :, :], mine, ALU.add)
                dve.drain()
                v.tensor_reduce(mean[:, :], hg2[:, :, :], AX, ALU.add)
                dve.drain()
                v.tensor_scalar(mean[:, :], mean[:, :], 1.0 / C, None, ALU.mult)
                dve.drain()
                v.tensor_tensor(hg2[:, :, :], hg2[:, :, :], mean[:, :, None].to_broadcast([P, GN, C]), ALU.subtract)
                dve.drain()
                v.tensor_tensor(sq[:, :, :], hg2[:, :, :], hg2[:, :, :], ALU.mult)
                dve.drain()
                v.tensor_reduce(var[:, :], sq[:, :, :], AX, ALU.add)
                dve.drain()
                v.tensor_scalar(var[:, :], var[:, :], 1.0 / C, LN_EPS, ALU.mult, ALU.add).then_inc(var_ready, 1)
                dve.wait_ge(dev_ready, i + 2)
                v.reciprocal(var[:, :], var[:, :])
                dve.drain()
                return v.tensor_tensor(target if target is not None else mine, hg2[:, :, :],
                                       var[:, :, None].to_broadcast([P, GN, C]), ALU.mult)

            def gat_pass(L):
                with dve.Fori(0, ITER) as it:
                    dve.drain()
                    dve.wait_ge(alpha_loaded, 16 * (L * ITER + it + 1))
                    v.tensor_copy(alpha_e[:, :, 0:1], alpha_e[:, :, JI:JI + 1])
                    dve.drain()
                    for h in range(H):
                        last = v.tensor_tensor_scan(alpha_e[:, h, 1:JI + 1], keep[:, bass.ds(it * JI, JI)],
                                                    alpha_raw[:, :, h], alpha_e[:, h, 0:1], ALU.mult, ALU.add)
                    last.then_inc(alpha_free, 1)
                    dve.drain()
                    for b in range(SLOTS):
                        K = L * CHUNKS + it * SLOTS + b
                        dve.wait_ge(gat_gathered[b], ONE_STEP * (L * ITER + it + 1))
                        v.tensor_tensor(logit0[:, :, :], slot_rows[:, b, :, C:C + 2].rearrange("p j h -> p h j"),
                                        alpha_e[:, :, 1 + b * J:1 + (b + 1) * J], ALU.add)
                        dve.drain()
                        v.scalar_tensor_tensor(logit[:, :, :], logit0[:, :, :], SLOPE1, logit0[:, :, :], ALU.mult, ALU.max)
                        dve.wait_ge(rows_staged, CHUNKS + K)
                        dve.sem_inc(dve_turn, 1)
                        v.tensor_copy(run_max[:, :, 0:1], run_max[:, :, J:J1])
                        v.tensor_copy(X3[:, :, 0:1], S3[:, :, J:J1])
                        dve.drain()
                        mask = reset[:, bass.ds(it * JI + b * J, J)]
                        for h in range(H):
                            v.tensor_tensor_scan(run_max[:, h, 1:J1], mask, logit[:, h, :], run_max[:, h, 0:1],
                                                 ALU.add, ALU.max)
                        dve.drain()
                        v.tensor_tensor(exps[:, 0, :, :], run_max[:, :, 0:J],
                                        mask[:, None, :].to_broadcast([P, H, J]), ALU.add)
                        v.tensor_tensor(exps[:, 1, :, :], logit[:, :, :], run_max[:, :, 1:J1], ALU.subtract)
                        dve.drain()
                        v.tensor_tensor(exps[:, 0, :, :], exps[:, 0, :, :], run_max[:, :, 1:J1], ALU.subtract)\
                            .then_inc(exps_in, 1)
                        dve.wait_ge(weights_ready, K + 1)
                        v.tensor_tensor(X4[:, :, 0:CH, 1:J1],
                                        slot_rows[:, b, :, 0:C].rearrange("p j (h c) -> p h c j", h=H),
                                        X4[:, :, CH:CH + 1, 1:J1].to_broadcast([P, H, CH, J]), ALU.mult)
                        dve.drain()
                        v.tensor_tensor_scan(S[:, :], F[:, :], X[:, :], 0.0, ALU.mult, ALU.add).then_inc(gat_sum, 1)
                        v.tensor_copy(ring_ids[:, b * J:(b + 1) * J], src_ids[:, bass.ds((it + 1) * JI + b * J, J)])\
                            .then_inc(slot_ready, 1)
                dve.drain()
                dve.wait_ge(rows_staged, CHUNKS + (L + 1) * CHUNKS)
                dve.sem_inc(dve_turn, 1)

            def node_groups(t, finish):
                dve.drain()
                put_ids(0, 0)
                with dve.Fori(0, PAIRS) as it:
                    for k in range(2):
                        finish(it, k)

            def after_conv(it, k):
                q = GROUPS + 2 * it + k
                node_means(0, it, k, q)
                layer_norm(2 * it + k, 2 * it + k, hg[:, :, :])
                dve.drain()
                v.tensor_copy(feats[:, bass.ds((2 * it + k) * GN, GN), :], hg[:, :, :]).then_inc(h_ready, 1)

            complete_first_rows(0)
            v.tensor_copy(wl[:, :], wcat[:, 0, :])
            node_groups(0, after_conv)
            gat_pass(0)

            with dve.Fori(1, LAYERS) as L:
                complete_first_rows(L)
                v.tensor_copy(wl[:, :], wcat[:, bass.ds(L, 1), :].rearrange("k a r -> k (a r)"))
                dve.drain()
                v.tensor_copy(bias_l[:, :], biasb[:, bass.ds(L - 1, 1), :].rearrange("p a c -> p (a c)"))

                def after_gat(it, k):
                    q = (L + 1) * GROUPS + 2 * it + k
                    node_means(L, it, k, q)
                    v.tensor_tensor(hg2[:, :, :], hg2[:, :, :], bias_l[:, None, :].to_broadcast([P, GN, C]), ALU.add)
                    dve.drain()
                    v.tensor_scalar(hg[:, :, :], hg2[:, :, :], 0.0, None, ALU.max).then_inc(h_ready, 1)

                node_groups(L, after_gat)
                gat_pass(L)

            complete_first_rows(LAYERS)

            def after_last(it, k):
                node_means(LAYERS, it, k, None)
                v.tensor_tensor(hg2[:, :, :], hg2[:, :, :], biasb[:, LAYERS - 1, None, :].to_broadcast([P, GN, C]), ALU.add)
                dve.drain()
                layer_norm(2 * it + k, GROUPS + 2 * it + k, None).then_inc(out_ready, 1)

            node_groups(LAYERS, after_last)


_WEIGHTS = ["L1_gnn_Ws", "L1_gnn_Wd", "L1_gnn_as", "L1_gnn_ad", "L1_gnn_b"]


def kernel(**inputs):
    import concourse.bacc as bacc
    from concourse.bass_utils import run_bass_kernel_spmd as run

    nc = bacc.Bacc("TRN2", target_bir_lowering=False, num_devices=1)
    arrays = {}

    def given(name):
        a = np.ascontiguousarray(inputs[name])
        arrays[name] = a
        return nc.dram_tensor(name, a.shape, mybir.dt.from_np(a.dtype), kind="ExternalInput").ap()

    first = [given(n) for n in ("x", "src", "dst", "L0_gnn_W", "L0_gnn_b", "L0_gnn_gamma", "L0_gnn_beta")]
    layers = [[given(f"{n}{l + 1}") for l in range(LAYERS)] for n in _WEIGHTS]
    out = nc.dram_tensor("out", (N, C), mybir.dt.float32, kind="ExternalOutput").ap()
    build(nc, *first, *layers, out)
    return run(nc, [arrays], core_ids=[0]).results[0]["out"]
```

```python
from contextlib import ExitStack

import numpy as np

import concourse.bass as bass
from concourse import mybir

P = 128
N, E, C, H, CH = 12500, 400000, 64, 2, 32
EPP = E // P
J = 25
SLOTS = 5
ITER = EPP // (J * SLOTS)
JI = J * SLOTS
CHUNKS = EPP // J
NPP = 98
NPAD = NPP * P
LASTN = N - (P - 1) * NPP
GN = 7
GROUPS = NPP // GN
PAIRS = GROUPS // 2
ROW = C + 4
SW = H * (CH + 1)
J1 = J + 1
QB, QS = 11, 3
QN = QB * QS
LAYERS = 3
BIG = 3.0e38
TINY = 1.0e-30
BN_EPS, LN_EPS = 1e-5, 1e-5
SLOPE0, SLOPE1 = 0.3, 0.2
ONE_STEP = J * 16


def build(nc, x, src, dst, W0, b0, gamma, beta, Ws, Wd, a_s, a_d, bias, out):
    f32, i32 = mybir.dt.float32, mybir.dt.int32
    ALU, ACT, AX = mybir.AluOpType, mybir.ActivationFunctionType, mybir.AxisListType.X
    ctx = ExitStack()
    with ctx:
        def sb(name, shape, dt=f32):
            return ctx.enter_context(nc.sbuf_tensor(name, shape, dt))

        def ps(name, shape):
            return ctx.enter_context(nc.psum_tensor(name, shape, f32))

        def sem(name):
            return ctx.enter_context(nc.semaphore(name))

        def dram(name, shape, dt=f32):
            return nc.dram_tensor(name, shape, dt, kind="Internal").ap()

        table = dram("table", (NPAD, ROW))
        dst_term = dram("dst_term", (NPAD, C))
        sums = dram("sums", (E, ROW))
        conv_dst = dram("conv_dst", (E + NPAD, C))
        gat_dst = dram("gat_dst", (E + NPAD, 2))
        msgs = dram("msgs", (CHUNKS, P, C * J))
        samples = dram("samples", (P, EPP // J))

        src_ids = sb("src_ids", [P, EPP + JI], i32)
        keep = sb("keep", [P, EPP])
        reset = sb("reset", [P, EPP])
        feats = sb("feats", [P, NPP, C])
        rows = sb("rows", [P, SLOTS * J * ROW])
        ring_ids = sb("ring_ids", [P, JI], i32)
        X = sb("X", [P, SW * J1])
        F = sb("F", [P, SW * J1])
        S = sb("S", [P, SW * J1])
        stage_rows = sb("stage_rows", [P, J, ROW])
        ein = sb("ein", [P, C * J])
        z = sb("z", [P, C * J])
        z2 = sb("z2", [P, C * J])
        run_max = sb("run_max", [P, H, J1])
        logit0 = sb("logit0", [P, H, J])
        logit = sb("logit", [P, H, J])
        exps = sb("exps", [P, 2, H, J])
        alpha_raw = sb("alpha_raw", [P, JI, 2])
        alpha_e = sb("alpha_e", [P, H, JI + 1])
        node_rows = sb("node_rows", [P, 2, GN * ROW])
        hg = sb("hg", [P, GN, C])
        hg2 = sb("hg2", [P, GN, C])
        rden = sb("rden", [P, GN, H])
        mean = sb("mean", [P, GN])
        var = sb("var", [P, GN])
        hT = sb("hT", [C, GN * P])
        tstage = sb("tstage", [P, 2, GN * ROW])
        astage = sb("astage", [P, 2, GN * C])
        end_ids = sb("end_ids", [P, NPP + 2 * GN], i32)
        start_ids = sb("start_ids", [P, NPP], i32)
        end_ring = sb("end_ring", [P, 2, GN], i32)
        start_ring = sb("start_ring", [P, 2, GN], i32)
        has = sb("has", [P, NPP])
        first_ids = sb("first_ids", [P, 1], i32)
        patch_ids = sb("patch_ids", [P, 1], i32)
        first_rows = sb("first_rows", [P, ROW])
        ident = sb("ident", [P, P])
        ones = sb("ones", [P, P])
        w0 = sb("w0", [C, 2 * C])
        rhs0 = sb("rhs0", [C, 2 * C])
        ws = sb("ws", [C, LAYERS, C])
        wd = sb("wd", [C, LAYERS, C])
        asb = sb("asb", [C, LAYERS, C])
        adb = sb("adb", [C, LAYERS, C])
        wcat = sb("wcat", [C, LAYERS, ROW])
        wl = sb("wl", [C, ROW])
        biasb = sb("biasb", [P, LAYERS, C])
        b0b = sb("b0b", [P, C])
        gammab = sb("gammab", [P, C])
        betab = sb("betab", [P, C])
        stat = sb("stat", [P, 2, C])
        part = sb("part", [P, 2, C])
        bn = sb("bn", [P, 2, C])
        bn_s = sb("bn_s", [P, C])
        bn_t = sb("bn_t", [P, C])
        prev_i = sb("prev_i", [P, 1], i32)
        flags = sb("flags", [P, 6])
        edge0 = sb("edge0", [P, 1], i32)
        sign = sb("sign", [P, C])
        tmp_end, tmp_none, tmp_start = (sb(n, [P, NPP]) for n in ("tmp_end", "tmp_none", "tmp_start"))
        sq = sb("sq", [P, GN, C])
        bias_l = sb("bias_l", [P, C])
        first_row = sb("first_row", [P, P])
        query = sb("query", [P, NPP + 1 + QN])
        count = sb("count", [P, NPP + 1])
        qi = sb("qi", [P, NPP + 1 + QN], i32)
        blk = sb("blk", [P, QN])
        sub = sb("sub", [P, QN])
        cnt = sb("cnt", [P, QB])
        blk_i = sb("blk_i", [P, QN], i32)
        sub_i = sb("sub_i", [P, QN], i32)
        reset_row = sb("reset_row", [SW, P])
        ends = sb("ends", [P, 2, SW])
        max_row = sb("max_row", [SW, P + 1])
        sum_row = sb("sum_row", [SW, P + 1])
        tail_row = sb("tail_row", [SW, 2, P])
        patch = sb("patch", [P, ROW])
        pmax = sb("pmax", [P, 3, SW])
        pexp = sb("pexp", [P, 2, SW])

        dst_i = rows[:, 0:EPP].bitcast(i32)
        D = rows[:, EPP:2 * EPP]
        samp = ein[:, 0:EPP // J]
        got2 = [rows[:, k * QB * P:(k + 1) * QB * P].rearrange("p (q k) -> p q k", k=P) for k in range(QS)]
        rest = rows[:, QS * QB * P:]
        cmp_b = rest[:, 0:QB * P].rearrange("p (q k) -> p q k", k=P)
        got3 = [rest[:, QB * P + k * QB * J:QB * P + (k + 1) * QB * J].bitcast(i32).rearrange("p (q k) -> p q k", k=J)
                for k in range(QS)]
        got3f = z2[:, 0:QB * J].rearrange("p (q k) -> p q k", k=J)

        slot_rows = rows[:, :].rearrange("p (s j r) -> p s j r", s=SLOTS, r=ROW)
        CW = SW * J1
        X2, F2, S2 = (rows[:, n * CW:(n + 1) * CW] for n in range(3))
        stage2 = rows[:, 3 * CW:3 * CW + J * ROW].rearrange("p (j r) -> p j r", r=ROW)
        in2 = rows[:, 3 * CW + J * ROW:3 * CW + J * ROW + C * J]
        conv_in, conv_u = (ein[:, :], in2), (z[:, :], z2[:, :])
        conv_x, conv_f, conv_s = (X[:, :], X2), (F[:, :], F2), (S[:, :], S2)
        conv_st = (stage_rows[:, :, :], stage2)

        X4 = X[:, :].rearrange("p (h c j) -> p h c j", h=H, j=J1)
        F4 = F[:, :].rearrange("p (h c j) -> p h c j", h=H, j=J1)
        S3 = S[:, :].rearrange("p (c j) -> p c j", j=J1)
        X3 = X[:, :].rearrange("p (c j) -> p c j", j=J1)
        F3 = F[:, :].rearrange("p (c j) -> p c j", j=J1)
        z3 = z[:, :].rearrange("p (c j) -> p c j", j=J)
        z23 = z2[:, :].rearrange("p (c j) -> p c j", j=J)
        ein_jc = ein[:, :].rearrange("p (j c) -> p j c", c=C)
        node4 = [node_rows[:, k, :].rearrange("p (n r) -> p n r", r=ROW) for k in range(2)]
        tst = [tstage[:, k, :].rearrange("p (n r) -> p n r", r=ROW) for k in range(2)]
        ast = [astage[:, k, :].rearrange("p (n r) -> p n r", r=C) for k in range(2)]

        pT = ps("pT", [P, 2, 512])
        pP = ps("pP", [P, 512])
        pA = ps("pA", [P, 512])
        pR = ps("pR", [P, 512])
        pB = ps("pB", [P, 512])
        pS = ps("pS", [P, 512])

        in_dst, in_prev, in_src, in_x, in_w0, in_w = (
            sem(n) for n in ("in_dst", "in_prev", "in_src", "in_x", "in_w0", "in_w"))
        zero_filled = sem("zero_filled")
        samples_in = sem("samples_in")
        searched2 = [sem(f"searched2_{k}") for k in range(QS)]
        searched3 = [sem(f"searched3_{k}") for k in range(QS)]
        table_written = [sem(f"table_written{k}") for k in range(2)]
        starts_scattered = [sem(f"starts_scattered{k}") for k in range(2)]
        firsts_gathered, firsts_written = sem("firsts_gathered"), sem("firsts_written")
        conv_gathered = [sem(f"conv_gathered{k}") for k in range(SLOTS)]
        gat_gathered = [sem(f"gat_gathered{k}") for k in range(SLOTS)]
        ein_loaded, msgs_stored = sem("ein_loaded"), sem("msgs_stored")
        sums_stored = [sem(f"sums_stored{k}") for k in range(2)]
        msgs_loaded = [sem(f"msgs_loaded{k}") for k in range(2)]
        terms_loaded = [sem(f"terms_loaded{k}") for k in range(2)]
        terms_scattered = [sem(f"terms_scattered{k}") for k in range(2)]
        alpha_loaded = sem("alpha_loaded")
        nodes_fetched = [sem(f"nodes_fetched{k}") for k in range(2)]
        patch_gathered, patch_scattered = sem("patch_gathered"), sem("patch_scattered")
        out_stored = sem("out_stored")
        zeros_ready, consts_ready, clears_done, conv_ready = (
            sem(n) for n in ("zeros_ready", "consts_ready", "clears_done", "conv_ready"))
        w0_T, w0_ready, wcat_ready = sem("w0_T"), sem("w0_ready"), sem("wcat_ready")
        dst_ready, firstrow_ready = sem("dst_ready"), sem("firstrow_ready")
        samples_ready = sem("samples_ready")
        search2_ready, search3_ready, ids_ready = sem("search2_ready"), sem("search3_ready"), sem("ids_ready")
        flag_ready, flag_T = sem("flag_ready"), sem("flag_T")
        pool_turn = sem("pool_turn")
        sp_turn, act_turn, pe_turn, dve_turn = (sem(n) for n in ("sp_turn", "act_turn", "pe_turn", "dve_turn"))
        h_ready, h_T, hT_ready, projected, staged = (
            sem(n) for n in ("h_ready", "h_T", "hT_ready", "projected", "staged"))
        stage_free = [sem(f"stage_free{k}") for k in range(2)]
        slot_ready = sem("slot_ready")
        ein_free, X_ready, X_free, z_ready, z_free = (
            sem(n) for n in ("ein_free", "X_ready", "X_free", "z_ready", "z_free"))
        stat_ready, stat_summed = sem("stat_ready"), sem("stat_summed")
        var_ready, dev_ready = sem("var_ready"), sem("dev_ready")
        bn_ready, bn_done, shifted, conv_u_free, conv_F, conv_sum, starts_ready, search_done = (
            sem(n) for n in ("bn_ready", "bn_done", "shifted", "conv_u_free", "conv_F", "conv_sum", "starts_ready",
                            "search_done"))
        rows_staged, sums_free = sem("rows_staged"), sem("sums_free")
        alpha_free = sem("alpha_free")
        exps_in, weights_ready, gat_sum = sem("exps_in"), sem("weights_ready"), sem("gat_sum")
        node_ids = sem("node_ids")
        ends_ready, ends_T, tail_in, tail_exp, carry_ready, carry_T, patch_ready = (
            sem(n) for n in ("ends_ready", "ends_T", "tail_in", "tail_exp", "carry_ready", "carry_T", "patch_ready"))
        out_ready = sem("out_ready")

        x_p = x[0:(P - 1) * NPP, :].rearrange("(p i) c -> p i c", i=NPP)
        out_p = out[0:(P - 1) * NPP, :].rearrange("(p i) c -> p i c", i=NPP)
        PARTS = ((0, 112), (112, P - 1))
        table_p = table.rearrange("(p i) r -> p i r", i=NPP)
        dterm_p = dst_term.rearrange("(p i) r -> p i r", i=NPP)
        sums_p = sums.rearrange("(p j) r -> p j r", j=EPP)
        convd_p = conv_dst[0:E, :].rearrange("(p j) r -> p (j r)", j=EPP)
        gatd_p = gat_dst[0:E, :].rearrange("(p j) r -> p j r", j=EPP)
        dst_p = dst.rearrange("(p j) -> p j", j=EPP)
        dst_blocks = dst.rearrange("(b k) -> b k", k=J)

        block = ctx.enter_context(nc.Block())

        @block.sync
        def _(sp):
            def held(s, v):
                sp.wait_ge(s, v)
                sp.sem_inc(sp_turn, 1)

            sp.dma_start(dst_i, dst_p).then_inc(in_dst, 16)
            sp.wait_ge(clears_done, 1)
            with nc.allow_non_contiguous_dma(reason="one id per partition"):
                sp.dma_start(prev_i[1:P, :], dst_p[0:P - 1, EPP - 1:EPP]).then_inc(in_prev, 16)
            sp.wait_ge(samples_ready, 1)
            sp.dma_start(samples, samp).then_inc(samples_in, 16)
            for lo, hi in PARTS:
                sp.dma_start(feats[lo:hi, :, :], x_p[lo:hi, :, :]).then_inc(in_x, 16)
            sp.dma_start(feats[P - 1:P, 0:LASTN, :], x[(P - 1) * NPP:N, :].rearrange("(a i) c -> a i c", a=1)).then_inc(in_x, 16)
            sp.dma_start(w0[:, :], W0).then_inc(in_w0, 16)
            for t, v in ((b0b, b0), (gammab, gamma), (betab, beta)):
                sp.dma_start(t[:, :], v.partition_broadcast(P)).then_inc(in_w0, 16)
            sp.dma_start(src_ids[:, 0:EPP], src.rearrange("(p j) -> p j", j=EPP)).then_inc(in_src, 16)
            sp.dma_start(src_ids[:, EPP:EPP + JI], src.rearrange("(p j) -> p j", j=EPP)[:, 0:JI]).then_inc(in_src, 16)
            for l in range(LAYERS):
                sp.dma_start(ws[:, l, :], Ws[l]).then_inc(in_w, 16)
                sp.dma_start(wd[:, l, :], Wd[l]).then_inc(in_w, 16)
                sp.dma_start(asb[:, l, :], a_s[l].rearrange("h c -> (h c)").partition_broadcast(C)).then_inc(in_w, 16)
                sp.dma_start(adb[:, l, :], a_d[l].rearrange("h c -> (h c)").partition_broadcast(C)).then_inc(in_w, 16)
                sp.dma_start(biasb[:, l, :], bias[l].partition_broadcast(P)).then_inc(in_w, 16)
            for k in range(2):
                sp.sem_inc(stage_free[k], 1)
            sp.sem_inc(z_free, 1)
            sp.sem_inc(sums_free, 2)
            sp.sem_inc(alpha_free, 1)

            def write_table(stage, h0):
                with sp.Fori(0, PAIRS) as it:
                    for k in range(2):
                        held(staged, 2 * (h0 + it) + k + 2)
                        sp.dma_start(table_p[:, bass.ds((2 * it + k) * GN, GN), :], tst[k]).then_inc(table_written[k], 16)
                        if stage == 0:
                            sp.dma_start(dterm_p[:, bass.ds((2 * it + k) * GN, GN), :], ast[k]).then_inc(table_written[k], 16)
                    for k in range(2):
                        done = h0 + it + 1
                        held(table_written[k], 32 * (it + 1) if stage == 0 else 16 * (done + PAIRS))
                        if stage > 0:
                            held(starts_scattered[k], 16 * GN * (done - PAIRS))
                        sp.sem_inc(stage_free[k], 1)

            write_table(0, 0)

            def load_terms(it, k):
                sp.dma_start(ast[k], dterm_p[:, bass.ds((2 * it + k) * GN, GN), :]).then_inc(terms_loaded[k], 16)

            for k in range(2):
                load_terms(0, k)
            with sp.Fori(1, PAIRS) as it:
                for k in range(2):
                    held(terms_scattered[k], 16 * GN * it)
                    load_terms(it, k)
            sp.wait_ge(firsts_gathered, 16)
            for k in range(2):
                sp.wait_ge(terms_scattered[k], 16 * GN * PAIRS)
            sp.dma_start(convd_p[:, 0:C], first_rows[:, 0:C]).then_inc(firsts_written, 16)
            sp.wait_ge(firsts_written, 16)

            with sp.Fori(0, CHUNKS) as c:
                held(ein_free, c + 1)
                sp.dma_start(ein[:, :], convd_p[:, bass.ds(c * (J * C), J * C)]).then_inc(ein_loaded, 16)
                held(z_ready, c + 1)
                sp.dma_start(msgs[bass.ds(c, 1), :, :].rearrange("a p n -> (a p) n"), z[:, :]).then_inc(msgs_stored, 16)
                held(msgs_stored, 16 * (c + 1))
                sp.sem_inc(z_free, 1)

            def load_msgs(c, k):
                sp.dma_start(conv_in[k], msgs[bass.ds(c, 1), :, :].rearrange("a p n -> (a p) n")).then_inc(msgs_loaded[k], 16)

            def store_sums(K, row0, k):
                held(rows_staged, K + 3)
                sp.dma_start(sums_p[:, bass.ds(row0, J), :], conv_st[k]).then_inc(sums_stored[k], 16)

            def sums_are_stored(k, uses):
                held(sums_stored[k], 16 * uses)
                sp.sem_inc(sums_free, 1)

            def conv_step(c, k, more):
                if more:
                    held(shifted, c + 1)
                    load_msgs(c + 2, k)
                store_sums(c, c * J, k)

            load_msgs(0, 0)
            sp.wait_ge(conv_ready, 1)
            load_msgs(1, 1)
            conv_step(0, 0, True)
            with sp.Fori(0, CHUNKS // 2 - 1) as it:
                conv_step(2 * it + 1, 1, True)
                sums_are_stored(0, it + 1)
                conv_step(2 * it + 2, 0, True)
                sums_are_stored(1, it + 1)
            conv_step(CHUNKS - 2, 1, False)
            sums_are_stored(0, CHUNKS // 2)
            conv_step(CHUNKS - 1, 0, False)
            sums_are_stored(1, CHUNKS // 2)
            sums_are_stored(0, CHUNKS // 2 + 1)

            def gat_layer(L):
                write_table(1, (L + 1) * PAIRS)
                held(firsts_gathered, 16 * (L + 2))
                with nc.allow_non_contiguous_dma(reason="two values per partition"):
                    sp.dma_start(gatd_p[:, 0:1, :].rearrange("p a r -> p (a r)"), first_rows[:, C + 2:ROW]).then_inc(firsts_written, 16)
                held(firsts_written, 16 * (L + 2))
                with sp.Fori(0, ITER) as it:
                    held(alpha_free, L * ITER + it + 1)
                    sp.dma_start(alpha_raw[:, :, :], gatd_p[:, bass.ds(it * JI, JI), :]).then_inc(alpha_loaded, 16)
                    for b in range(SLOTS):
                        K = (L + 1) * CHUNKS + it * SLOTS + b
                        store_sums(K, it * JI + b * J, 0)
                        sums_are_stored(0, K + 1 - CHUNKS // 2)

            with sp.Fori(0, LAYERS) as L:
                gat_layer(L)

            half = NPP // 2
            for n, (a, b) in enumerate(((0, half), (half, NPP))):
                sp.wait_ge(out_ready, (n + 1) * GROUPS // 2)
                for lo, hi in PARTS:
                    sp.dma_start(out_p[lo:hi, a:b, :], feats[lo:hi, a:b, :]).then_inc(out_stored, 16)
                e = min(b, LASTN)
                sp.dma_start(out[(P - 1) * NPP + a:(P - 1) * NPP + e, :].rearrange("(a i) c -> a i c", a=1),
                             feats[P - 1:P, a:e, :]).then_inc(out_stored, 16)
            sp.wait_ge(out_stored, 96)

        @block.gpsimd
        def _(pool):
            def at(col):
                return bass.IndirectOffsetOnAxis(ap=col, axis=0)

            def gather(out_, table_, col):
                return pool.indirect_dma_start(out=out_, out_offset=None, in_=table_, in_offset=at(col))

            def scatter(table_, col, in_):
                return pool.indirect_dma_start(out=table_, out_offset=at(col), in_=in_, in_offset=None)

            pool.memset(ident[:, :], 0.0)
            pool.iota(qi[:, :], pattern=[[1, NPP + 1 + QN]], base=-1, channel_multiplier=NPP)
            pool.iota(edge0[:, :], pattern=[[1, 1]], base=0, channel_multiplier=EPP)
            pool.drain()
            pool.affine_select(out=ident[:, :], in_=ident[:, :], compare_op=ALU.not_equal, fill=1.0, base=0,
                               pattern=[[-1, P]], channel_multiplier=1).then_inc(consts_ready, 1)

            pool.wait_ge(samples_in, 16)
            def zero_fill(n):
                pool.dma_start(convd_p[:, bass.ds(n * (JI * C), JI * C)].rearrange("p (a n) -> p a n", a=SLOTS),
                               z[:, None, :].to_broadcast([P, SLOTS, J * C])).then_inc(zero_filled, 16)

            FILLS = 6
            pool.wait_ge(zeros_ready, 1)
            with pool.Fori(0, (NPP + 1) // QN) as it:
                for k in range(QS):
                    pool.wait_ge(search2_ready, it * QS + k + 1)
                    pool.sem_inc(pool_turn, 1)
                    for q in range(QB):
                        gather(got2[k][:, q, 0:EPP // J], samples, blk_i[:, k * QB + q:k * QB + q + 1]).then_inc(searched2[k], 16)
                for n in range(3):
                    zero_fill(it * FILLS + n)
                for k in range(QS):
                    pool.wait_ge(search3_ready, it * QS + k + 1)
                    pool.sem_inc(pool_turn, 1)
                    for q in range(QB):
                        gather(got3[k][:, q, :], dst_blocks, sub_i[:, k * QB + q:k * QB + q + 1]).then_inc(searched3[k], 16)
                for n in range(3, FILLS):
                    zero_fill(it * FILLS + n)
            pool.dma_start(gatd_p[:, :, :].rearrange("p (a j) r -> p a (j r)", a=5),
                           z[:, None, 0:EPP * 2 // 5].to_broadcast([P, 5, EPP * 2 // 5])).then_inc(zero_filled, 16)

            def scatter_starts(k, target, values, scattered):
                for n in range(GN):
                    scatter(target, start_ring[:, k, n:n + 1], values[:, n, :]).then_inc(scattered[k], 16)

            def table_done(uses):
                for k in range(2):
                    pool.wait_ge(stage_free[k], uses + 1)
                pool.sem_inc(pool_turn, 1)

            def gather_firsts(source, width):
                gather(first_rows[:, 0:width], source, first_ids[:, 0:1]).then_inc(firsts_gathered, 16)

            def edge_turn(gathered, K0, it, fills=()):
                for b in range(SLOTS):
                    pool.wait_ge(slot_ready, K0 + it * SLOTS + b + 1)
                    pool.sem_inc(pool_turn, 1)
                    for j in range(J):
                        gather(slot_rows[:, b, j, :], table, ring_ids[:, b * J + j:b * J + j + 1])\
                            .then_inc(gathered[b], 16)
                    for n in fills[b::SLOTS]:
                        zero_fill(n)

            def complete_first_rows(t):
                pool.wait_ge(sums_free, (t + 1) * CHUNKS + 2)
                pool.sem_inc(pool_turn, 1)
                gather(patch[:, :], sums, patch_ids[:, 0:1]).then_inc(patch_gathered, 16)
                pool.wait_ge(patch_ready, t + 1)
                pool.sem_inc(pool_turn, 1)
                scatter(sums, patch_ids[:, 0:1], patch[:, :]).then_inc(patch_scattered, 16)
                pool.wait_ge(patch_scattered, 16 * (t + 1))
                pool.sem_inc(pool_turn, 1)

            def fetch_nodes(t, it, k):
                pool.wait_ge(node_ids, t * (GROUPS + 2) + 2 * it + k + 1)
                pool.sem_inc(pool_turn, 1)
                for n in range(GN):
                    gather(node4[k][:, n, :], sums, end_ring[:, k, n:n + 1]).then_inc(nodes_fetched[k], 16)

            table_done(PAIRS)
            pool.wait_ge(search_done, 1)
            gather_firsts(dst_term, C)
            edge_turn(conv_gathered, 0, 0, range(FILLS * ((NPP + 1) // QN), ITER))
            pool.wait_ge(zero_filled, 16 * (ITER + 1))
            with pool.Fori(0, PAIRS) as it:
                for k in range(2):
                    pool.wait_ge(terms_loaded[k], 16 * (it + 1))
                    pool.sem_inc(pool_turn, 1)
                    pool.wait_ge(starts_ready, 2 * it + k + 1)
                    pool.sem_inc(pool_turn, 1)
                    scatter_starts(k, conv_dst, ast[k], terms_scattered)
            with pool.Fori(1, ITER) as it:
                edge_turn(conv_gathered, 0, it)

            def shift(c, k, n):
                pool.wait_ge(msgs_loaded[k], 16 * (n + 1))
                pool.sem_inc(pool_turn, 1)
                pool.wait_ge(conv_u_free, c + 1)
                pool.tensor_tensor(conv_u[k].rearrange("p (c j) -> p c j", j=J),
                                   conv_in[k].rearrange("p (c j) -> p c j", j=J),
                                   bn_t[:, :, None].to_broadcast([P, C, J]), ALU.add).then_inc(shifted, 1)

            pool.wait_ge(conv_ready, 1)
            with pool.Fori(0, CHUNKS // 2) as it:
                for k in range(2):
                    shift(2 * it + k, k, it)
            shift(CHUNKS - 1, 0, CHUNKS // 2)

            with pool.Fori(0, LAYERS) as L:
                complete_first_rows(L)
                def scatter_alphas(it, k):
                    pool.wait_ge(staged, (L + 1) * GROUPS + 2 * it + k + 2)
                    pool.sem_inc(pool_turn, 1)
                    scatter_starts(k, gat_dst, tst[k][:, :, C + 2:ROW], starts_scattered)

                for k in range(2):
                    fetch_nodes(L, 0, k)
                with pool.Fori(0, PAIRS - 1) as it:
                    for k in range(2):
                        fetch_nodes(L, it + 1, k)
                        scatter_alphas(it, k)
                for k in range(2):
                    scatter_alphas(PAIRS - 1, k)
                table_done((L + 2) * PAIRS)
                gather_firsts(table, ROW)
                with pool.Fori(0, ITER) as it:
                    edge_turn(gat_gathered, (L + 1) * CHUNKS, it)
            complete_first_rows(LAYERS)
            with pool.Fori(0, PAIRS) as it:
                for k in range(2):
                    fetch_nodes(LAYERS, it, k)

        @block.scalar
        def _(act):
            def held(s, v):
                act.wait_ge(s, v)
                act.sem_inc(act_turn, 1)

            act.sem_inc(staged, 1)
            act.sem_inc(ein_free, 1)
            act.sem_inc(rows_staged, 2)
            act.wait_ge(in_x, 48)

            def project(stage, h0):
                with act.Fori(0, PAIRS) as it:
                    for k in range(2):
                        q = 2 * (h0 + it) + k
                        if stage == 0:
                            held(h_T, q + 1)
                            nc.scalar.copy(hg[:, :, :], feats[:, bass.ds(q * GN, GN), :]).then_inc(h_ready, 1)
                        if stage == 1:
                            deviation(2 * it + k)
                        act.wait_ge(h_T, q + 2)
                        nc.scalar.copy(hT[:, 0:4 * P], pT[0:C, 0, 0:4 * P])
                        nc.scalar.copy(hT[:, 4 * P:GN * P], pT[0:C, 1, 0:3 * P]).then_inc(hT_ready, 1)
                        act.wait_ge(projected, q + 1)
                        act.sem_inc(act_turn, 1)
                        held(stage_free[k], h0 + it + 1)
                        if stage > 0:
                            nc.scalar.copy(start_ring[:, k, :], start_ids[:, bass.ds((2 * it + k) * GN, GN)])
                        else:
                            nc.scalar.copy(ast[k], pA[:, 0:GN * C].rearrange("p (n r) -> p n r", r=C))
                        nc.scalar.copy(tst[k], pP[:, 0:GN * ROW].rearrange("p (n r) -> p n r", r=ROW)).then_inc(staged, 1)

            def deviation(i):
                act.wait_ge(var_ready, i + 1)
                nc.scalar.activation(var[:, :], var[:, :], ACT.Sqrt).then_inc(dev_ready, 1)

            def tails(t):
                act.wait_ge(tail_in, 2 * t + 1)
                nc.scalar.activation(tail_row[:, :, :], tail_row[:, :, :], ACT.Exp).then_inc(tail_exp, 1)
                act.wait_ge(tail_in, 2 * t + 2)
                nc.scalar.activation(pexp[:, :, :], pexp[:, :, :], ACT.Exp).then_inc(tail_exp, 1)

            project(0, 0)
            act.wait_ge(ids_ready, 1)
            for k in range(2):
                nc.scalar.copy(start_ring[:, k, :], start_ids[:, k * GN:(k + 1) * GN]).then_inc(starts_ready, 1)
            with act.Fori(1, PAIRS) as it:
                for k in range(2):
                    held(terms_scattered[k], 16 * GN * it)
                    nc.scalar.copy(start_ring[:, k, :], start_ids[:, bass.ds((2 * it + k) * GN, GN)]).then_inc(starts_ready, 1)
            with act.Fori(0, CHUNKS) as c:
                act.wait_ge(ein_loaded, 16 * (c + 1))
                act.sem_inc(act_turn, 1)
                held(X_free, c + 1)
                nc.scalar.copy(F3[:, 0:C, 1:J1], keep[:, None, bass.ds(c * J, J)].to_broadcast([P, C, J]))
                nc.scalar.copy(X3[:, 0:C, 1:J1], ein_jc.rearrange("p j c -> p c j")).then_inc(X_ready, 1)
                act.drain().then_inc(ein_free, 1)

            act.wait_ge(bn_ready, 1)
            nc.scalar.activation(part[:, 0, :], part[:, 0, :], ACT.Sqrt).then_inc(dev_ready, 1)
            def decay(c, k):
                held(conv_sum, c + 1)
                nc.scalar.copy(conv_f[k].rearrange("p (c j) -> p c j", j=J1)[:, :, 1:J1],
                               keep[:, None, bass.ds(c * J, J)].to_broadcast([P, SW, J])).then_inc(conv_F, 1)

            def stage_sums(c, k):
                act.wait_ge(conv_sum, c + 3)
                act.sem_inc(act_turn, 1)
                act.wait_ge(sums_free, c + 1)
                nc.scalar.copy(conv_st[k][:, :, 0:SW],
                               conv_s[k].rearrange("p (c j) -> p j c", j=J1)[:, 1:J1, :]).then_inc(rows_staged, 1)

            act.wait_ge(conv_ready, 1)
            decay(0, 0)
            with act.Fori(0, CHUNKS // 2) as it:
                for k in range(2):
                    decay(2 * it + k + 1, 1 - k)
                    stage_sums(2 * it + k, k)
            stage_sums(CHUNKS - 1, 0)

            def gat_pass(L):
                with act.Fori(0, ITER) as it:
                    for b in range(SLOTS):
                        K = L * CHUNKS + it * SLOTS + b
                        act.wait_ge(exps_in, K + 1)
                        for h in range(H):
                            nc.scalar.activation(F4[:, h, :, 1:J1],
                                                 exps[:, 0, h, None, :].to_broadcast([P, CH + 1, J]), ACT.Exp)
                        nc.scalar.activation(X4[:, :, CH, 1:J1], exps[:, 1, :, :], ACT.Exp).then_inc(weights_ready, 1)
                        act.wait_ge(gat_sum, K + 1)
                        act.sem_inc(act_turn, 1)
                        act.wait_ge(sums_free, CHUNKS + K + 2)
                        nc.scalar.copy(stage_rows[:, :, SW:ROW], run_max[:, :, 1:J1].rearrange("p h j -> p j h"))
                        nc.scalar.copy(stage_rows[:, :, 0:SW], S3[:, :, 1:J1].rearrange("p c j -> p j c")).then_inc(rows_staged, 1)
            tails(0)
            project(1, PAIRS)
            gat_pass(0)
            with act.Fori(1, LAYERS) as L:
                tails(L)
                project(2, (L + 1) * PAIRS)
                gat_pass(L)
            tails(LAYERS)
            with act.Fori(0, GROUPS) as g:
                deviation(GROUPS + g)

        @block.tensor
        def _(pe):
            pe.wait_ge(in_w0, 64)
            pe.wait_ge(consts_ready, 1)
            for k in range(2):
                last = nc.tensor.transpose(pT[0:C, 0, k * C:(k + 1) * C], w0[:, k * C:(k + 1) * C], ident[0:C, 0:C])
            last.then_inc(w0_T, 1)
            pe.wait_ge(dst_ready, 1)
            nc.tensor.matmul(pR[:, 0:P], first_row[:, :], ident[:, :], start=True, stop=True).then_inc(firstrow_ready, 1)
            pe.wait_ge(flag_ready, 1)
            nc.tensor.transpose(pR[0:SW, 0:P], ends[:, 0, :], ident[:, :]).then_inc(flag_T, 1)
            pe.sem_inc(h_T, 1)
            pe.wait_ge(w0_ready, 1)

            def project(stage, h0):
                with pe.Fori(0, PAIRS) as it:
                    for k in range(2):
                        q = 2 * (h0 + it) + k
                        pe.wait_ge(h_ready, q + 1)
                        pe.sem_inc(pe_turn, 1)
                        for n in range(GN):
                            last = nc.tensor.transpose(pT[0:C, n // 4, (n % 4) * P:(n % 4 + 1) * P], hg[:, n, :], ident[:, :])
                        last.then_inc(h_T, 1)
                        pe.wait_ge(staged, q + 1)
                        pe.sem_inc(pe_turn, 1)
                        pe.wait_ge(hT_ready, q + 1)
                        for n in range(GN):
                            lhsT = hT[:, n * P:(n + 1) * P]
                            if stage == 0:
                                nc.tensor.matmul(pA[:, n * C:(n + 1) * C], lhsT, rhs0[:, C:2 * C], start=True, stop=True)
                            last = nc.tensor.matmul(pP[:, n * ROW:(n + 1) * ROW], lhsT, wl[:, :], start=True, stop=True)
                        last.then_inc(projected, 1)

            def tails(t):
                pe.wait_ge(ends_ready, t + 1)
                pe.sem_inc(pe_turn, 1)
                for k in range(2):
                    last = nc.tensor.transpose(pR[0:SW, k * P:(k + 1) * P], ends[:, k, :], ident[:, :])
                last.then_inc(ends_T, 1)
                pe.wait_ge(carry_ready, t + 1)
                pe.sem_inc(pe_turn, 1)
                nc.tensor.transpose(pB[:, 0:SW], sum_row[:, 0:P], ident[0:SW, 0:SW])
                nc.tensor.transpose(pB[:, P:P + SW], max_row[:, 0:P], ident[0:SW, 0:SW]).then_inc(carry_T, 1)

            project(0, 0)
            pe.wait_ge(stat_ready, 1)
            nc.tensor.matmul(pS[:, 0:2 * C], ones[:, :], stat[:, :, :].rearrange("p a c -> p (a c)"),
                             start=True, stop=True).then_inc(stat_summed, 1)
            with pe.Fori(0, LAYERS) as L:
                tails(L)
                project(1, (L + 1) * PAIRS)
            tails(LAYERS)

        @block.vector
        def _(dve):
            v = nc.vector

            def bc(ap, shape):
                return ap.to_broadcast(shape)

            v.memset(z[:, :], 0.0).then_inc(zeros_ready, 1)
            v.memset(prev_i[:, :], -1)
            v.memset(feats[96:P, LASTN:NPP, :], 0.0)
            dve.drain().then_inc(clears_done, 1)
            v.memset(ones[:, :], 1.0)
            dve.wait_ge(in_dst, 16)
            v.tensor_copy(D, dst_i)
            dve.drain()
            v.tensor_copy(samp, D[:, 0:EPP:J]).then_inc(samples_ready, 1)
            v.tensor_copy(first_row[:, :], bc(D[:, 0:1], [P, P])).then_inc(dst_ready, 1)
            v.tensor_copy(first_ids[:, :], D[:, 0:1])
            v.tensor_tensor(keep[:, 1:EPP], D[:, 1:EPP], D[:, 0:EPP - 1], ALU.is_equal)
            v.memset(keep[:, 0:1], 0.0)
            v.tensor_scalar(reset[:, :], D, D[:, 0:1], None, ALU.is_equal)
            v.tensor_tensor(flags[:, 1:2], D[:, 0:1], D[:, EPP - 1:EPP], ALU.is_equal)
            dve.wait_ge(in_prev, 16)
            v.tensor_copy(flags[:, 4:5], prev_i[:, :])
            dve.wait_ge(consts_ready, 1)
            v.tensor_copy(query[:, :], qi[:, :])
            dve.drain()
            v.tensor_tensor(flags[:, 0:1], D[:, 0:1], flags[:, 4:5], ALU.is_equal)
            v.tensor_reduce(flags[:, 2:3], reset[:, :], AX, ALU.add)
            dve.drain()
            v.tensor_tensor(flags[:, 3:4], flags[:, 0:1], flags[:, 1:2], ALU.mult)
            v.tensor_scalar(reset[:, :], keep[:, :], BIG, BIG, ALU.mult, ALU.subtract)
            v.tensor_copy(flags[:, 5:6], edge0[:, :])
            dve.drain()
            v.scalar_tensor_tensor(flags[:, 4:5], flags[:, 2:3], -1.0, flags[:, 5:6], ALU.add, ALU.add)
            v.tensor_scalar(flags[:, 3:4], flags[:, 3:4], BIG, BIG, ALU.mult, ALU.subtract)
            v.tensor_scalar(flags[:, 0:1], flags[:, 0:1], BIG, BIG, ALU.mult, ALU.subtract)
            dve.drain()
            v.tensor_copy(patch_ids[:, :], flags[:, 4:5])

            def among_firsts(base, k):
                mine = query[:, bass.ds(base + k * QB, QB)]
                my = slice(k * QB, (k + 1) * QB)
                v.tensor_tensor(cmp_b, mine[:, :, None].to_broadcast([P, QB, P]),
                                first_row[:, None, :].to_broadcast([P, QB, P]), ALU.is_ge)
                dve.drain()
                v.tensor_reduce(cnt[:, :], cmp_b, AX, ALU.add)
                dve.drain()
                v.tensor_scalar(blk[:, my], cnt[:, :], -1.0, 0.0, ALU.add, ALU.max)
                dve.drain()
                v.tensor_copy(blk_i[:, my], blk[:, my]).then_inc(search2_ready, 1)

            def among_samples(base, it, k):
                mine = query[:, bass.ds(base + k * QB, QB)]
                my = slice(k * QB, (k + 1) * QB)
                dve.wait_ge(searched2[k], 16 * QB * (it + 1))
                v.tensor_tensor(cmp_b[:, :, 0:EPP // J], mine[:, :, None].to_broadcast([P, QB, EPP // J]),
                                got2[k][:, :, 0:EPP // J], ALU.is_ge)
                dve.drain()
                v.tensor_reduce(cnt[:, :], cmp_b[:, :, 0:EPP // J], AX, ALU.add)
                dve.drain()
                v.tensor_scalar(cnt[:, :], cnt[:, :], -1.0, 0.0, ALU.add, ALU.max)
                dve.drain()
                v.scalar_tensor_tensor(sub[:, my], blk[:, my], float(EPP // J), cnt[:, :], ALU.mult, ALU.add)
                dve.drain()
                v.tensor_copy(sub_i[:, my], sub[:, my]).then_inc(search3_ready, 1)

            def among_ids(base, it, k):
                mine = query[:, bass.ds(base + k * QB, QB)]
                my = slice(k * QB, (k + 1) * QB)
                dve.wait_ge(searched3[k], 16 * QB * (it + 1))
                v.tensor_copy(got3f, got3[k])
                dve.drain()
                v.tensor_tensor(cmp_b[:, :, 0:J], mine[:, :, None].to_broadcast([P, QB, J]), got3f, ALU.is_ge)
                dve.drain()
                v.tensor_reduce(cnt[:, :], cmp_b[:, :, 0:J], AX, ALU.add)
                dve.drain()
                v.scalar_tensor_tensor(count[:, bass.ds(base + k * QB, QB)], sub[:, my], float(J), cnt[:, :],
                                       ALU.mult, ALU.add)
                dve.drain()

            dve.wait_ge(in_src, 32)
            v.tensor_copy(ring_ids[:, :], src_ids[:, 0:JI]).then_inc(slot_ready, SLOTS)
            dve.wait_ge(firstrow_ready, 1)
            v.tensor_copy(first_row[:, :], pR[:, 0:P])
            dve.drain()
            v.tensor_copy(ends[:, 0, :], bc(flags[:, 3:4], [P, SW])).then_inc(flag_ready, 1)
            for k in range(QS):
                among_firsts(0, k)
            dve.wait_ge(in_w0, 64)
            v.tensor_scalar(sign[:, :], gammab[:, :], 0.0, None, ALU.is_ge)
            dve.drain()
            v.tensor_scalar(sign[:, :], sign[:, :], 2.0, 1.0, ALU.mult, ALU.subtract)
            dve.drain()
            dve.wait_ge(w0_T, 1)
            v.tensor_tensor(rhs0[:, 0:C], pT[0:C, 0, C:2 * C], sign[0:C, :], ALU.mult)
            v.tensor_tensor(rhs0[:, C:2 * C], pT[0:C, 0, 0:C], sign[0:C, :], ALU.mult)
            v.memset(wl[:, C:ROW], 0.0)
            dve.drain()
            v.tensor_copy(wl[:, 0:C], rhs0[:, 0:C])
            v.tensor_tensor(rhs0[:, C:2 * C], rhs0[:, C:2 * C], rhs0[:, 0:C], ALU.subtract).then_inc(w0_ready, 1)
            with dve.Fori(0, (NPP + 1) // QN) as it:
                for k in range(QS):
                    among_samples(it * QN, it, k)
                for k in range(QS):
                    among_firsts(it * QN + QN, k)
                for k in range(QS):
                    among_ids(it * QN, it, k)
            dve.drain().then_inc(search_done, 1)
            v.tensor_tensor(has[:, :], count[:, 1:NPP + 1], count[:, 0:NPP], ALU.is_gt)
            v.tensor_scalar(tmp_end[:, :], count[:, 1:NPP + 1], -1.0, 0.0, ALU.add, ALU.max)
            v.tensor_scalar(tmp_none[:, :], query[:, 1:NPP + 1], float(E), None, ALU.add)
            dve.drain()
            v.memset(end_ids[:, NPP:NPP + 2 * GN], 0.0)
            v.tensor_copy(end_ids[:, 0:NPP], tmp_end[:, :])
            v.tensor_tensor(tmp_start[:, :], count[:, 0:NPP], tmp_none[:, :], ALU.subtract)
            dve.drain()
            v.tensor_tensor(tmp_start[:, :], tmp_start[:, :], has[:, :], ALU.mult)
            dve.drain()
            v.tensor_tensor(tmp_start[:, :], tmp_start[:, :], tmp_none[:, :], ALU.add)
            dve.drain()
            v.tensor_copy(start_ids[:, :], tmp_start[:, :]).then_inc(ids_ready, 1)

            dve.wait_ge(flag_T, 1)
            v.tensor_copy(reset_row[:, :], pR[0:SW, 0:P])
            dve.wait_ge(in_w, 16 * 5 * LAYERS)
            v.tensor_tensor(asb[:, :, :], ws[:, :, :], asb[:, :, :], ALU.mult)
            v.tensor_tensor(adb[:, :, :], wd[:, :, :], adb[:, :, :], ALU.mult)
            v.tensor_copy(wcat[:, :, 0:C], ws[:, :, :])
            dve.drain()
            v.tensor_reduce(wcat[:, :, C:C + 2], asb[:, :, :].rearrange("k l (h c) -> k l h c", h=H), AX, ALU.add)
            v.tensor_reduce(wcat[:, :, C + 2:ROW], adb[:, :, :].rearrange("k l (h c) -> k l h c", h=H), AX, ALU.add)

            for buf in (X, F, S, max_row, sum_row):
                v.memset(buf[:, :], 0.0)
            for buf in (run_max, alpha_e, stat):
                v.memset(buf[:, :, :], 0.0)
            v.memset(stage_rows[:, :, :], 0.0)
            dve.drain().then_inc(X_free, 1)

            with dve.Fori(0, ITER) as it:
                for b in range(SLOTS):
                    c = it * SLOTS + b
                    dve.wait_ge(X_ready, c + 1)
                    v.tensor_copy(X3[:, 0:C, 0:1], S3[:, 0:C, J:J1])
                    dve.drain()
                    v.tensor_tensor_scan(S[:, 0:C * J1], F[:, 0:C * J1], X[:, 0:C * J1], 0.0, ALU.mult, ALU.add)\
                        .then_inc(X_free, 1)
                    dve.drain()
                    dve.wait_ge(conv_gathered[b], ONE_STEP * (it + 1))
                    dve.sem_inc(dve_turn, 1)
                    dve.wait_ge(z_free, c + 1)
                    v.tensor_tensor(z3, S3[:, 0:C, 1:J1], slot_rows[:, b, :, 0:C].rearrange("p j c -> p c j"),
                                    ALU.add).then_inc(z_ready, 1)
                    dve.drain()
                    v.tensor_copy(ring_ids[:, b * J:(b + 1) * J], src_ids[:, bass.ds((it + 1) * JI + b * J, J)])\
                        .then_inc(slot_ready, 1)
                    v.tensor_tensor(z2[:, :], z[:, :], z[:, :], ALU.mult)
                    v.tensor_reduce(part[:, 0, :], z3, AX, ALU.add)
                    dve.drain()
                    v.tensor_reduce(part[:, 1, :], z23, AX, ALU.add)
                    dve.drain()
                    v.tensor_tensor(stat[:, :, :], stat[:, :, :], part[:, :, :], ALU.add)
            dve.drain().then_inc(stat_ready, 1)

            dve.wait_ge(stat_summed, 1)
            v.tensor_scalar(bn[:, :, :].rearrange("p a c -> p (a c)"), pS[:, 0:2 * C], 1.0 / E, None, ALU.mult)
            v.tensor_tensor(b0b[:, :], b0b[:, :], sign[:, :], ALU.mult)
            v.tensor_tensor(gammab[:, :], gammab[:, :], sign[:, :], ALU.mult)
            dve.drain()
            v.tensor_tensor(part[:, 0, :], bn[:, 0, :], bn[:, 0, :], ALU.mult)
            v.tensor_tensor(part[:, 1, :], bn[:, 0, :], b0b[:, :], ALU.add)
            dve.drain()
            v.tensor_tensor(part[:, 0, :], bn[:, 1, :], part[:, 0, :], ALU.subtract)
            v.tensor_tensor(part[:, 1, :], b0b[:, :], part[:, 1, :], ALU.subtract)
            dve.drain()
            v.tensor_scalar(part[:, 0, :], part[:, 0, :], 0.0, BN_EPS, ALU.max, ALU.add)
            dve.drain().then_inc(bn_ready, 1)
            dve.wait_ge(dev_ready, 1)
            v.reciprocal(part[:, 0, :], part[:, 0, :])
            dve.drain()
            v.tensor_tensor(bn_s[:, :], part[:, 0, :], gammab[:, :], ALU.mult)
            dve.drain()
            v.tensor_scalar(bn_s[:, :], bn_s[:, :], TINY, None, ALU.max)
            dve.drain()
            v.reciprocal(part[:, 0, :], bn_s[:, :])
            dve.drain()
            v.tensor_tensor(part[:, 0, :], part[:, 0, :], betab[:, :], ALU.mult)
            dve.drain()
            v.tensor_tensor(bn_t[:, :], part[:, 1, :], part[:, 0, :], ALU.add)
            for buf in (F2, S2):
                v.memset(buf, 0.0)
            v.memset(stage2, 0.0)
            for buf in conv_x:
                v.memset(buf.rearrange("p (h c j) -> p h c j", h=H, j=J1)[:, :, CH, :], 1.0)
            dve.drain().then_inc(conv_ready, 1)
            dve.sem_inc(conv_sum, 2)
            dve.sem_inc(conv_u_free, 2)

            def conv_step(c, k):
                xk, other = conv_x[k], conv_s[1 - k]
                x4 = xk.rearrange("p (h c j) -> p h c j", h=H, j=J1)
                u3 = conv_u[k].rearrange("p (c j) -> p c j", j=J)
                v.tensor_copy(xk.rearrange("p (c j) -> p c j", j=J1)[:, :, 0:1],
                              other.rearrange("p (c j) -> p c j", j=J1)[:, :, J:J1])
                dve.wait_ge(shifted, c + 1)
                for h in range(H):
                    uh = u3[:, h * CH:(h + 1) * CH, :]
                    last = v.scalar_tensor_tensor(x4[:, h, 0:CH, 1:J1], uh, SLOPE0, uh, ALU.mult, ALU.max)
                last.then_inc(conv_u_free, 1)
                dve.drain()
                dve.wait_ge(rows_staged, c + 1)
                dve.sem_inc(dve_turn, 1)
                dve.wait_ge(conv_F, c + 1)
                v.tensor_tensor_scan(conv_s[k], conv_f[k], xk, 0.0, ALU.mult, ALU.add).then_inc(conv_sum, 1)
                dve.drain()

            with dve.Fori(0, CHUNKS // 2) as it:
                for k in range(2):
                    conv_step(2 * it + k, k)
            conv_step(CHUNKS - 1, 0)
            dve.wait_ge(rows_staged, CHUNKS + 2)
            dve.sem_inc(dve_turn, 1)

            def complete_first_rows(t):
                last_row = stage_rows[:, J - 1, :]
                v.tensor_copy(ends[:, 0, :], last_row[:, 0:SW])
                for h in range(H):
                    last = v.tensor_copy(ends[:, 1, h * (CH + 1):(h + 1) * (CH + 1)],
                                         bc(last_row[:, SW + h:SW + h + 1], [P, CH + 1]))
                last.then_inc(ends_ready, 1)
                dve.wait_ge(ends_T, t + 1)
                v.tensor_tensor_scan(max_row[:, 1:P + 1], reset_row[:, :], pR[0:SW, P:2 * P], 0.0, ALU.add, ALU.max)
                dve.drain()
                v.tensor_tensor(tail_row[:, 0, :], max_row[:, 0:P], reset_row[:, :], ALU.add)
                v.tensor_tensor(tail_row[:, 1, :], pR[0:SW, P:2 * P], max_row[:, 1:P + 1], ALU.subtract)
                dve.drain()
                v.tensor_tensor(tail_row[:, 0, :], tail_row[:, 0, :], max_row[:, 1:P + 1], ALU.subtract).then_inc(tail_in, 1)
                dve.wait_ge(tail_exp, 2 * t + 1)
                v.tensor_tensor(tail_row[:, 1, :], tail_row[:, 1, :], pR[0:SW, 0:P], ALU.mult)
                dve.drain()
                v.tensor_tensor_scan(sum_row[:, 1:P + 1], tail_row[:, 0, :], tail_row[:, 1, :], 0.0, ALU.mult, ALU.add)\
                    .then_inc(carry_ready, 1)
                dve.wait_ge(patch_gathered, 16 * (t + 1))
                for h in range(H):
                    v.tensor_copy(pmax[:, 0, h * (CH + 1):(h + 1) * (CH + 1)],
                                  bc(patch[:, SW + h:SW + h + 1], [P, CH + 1]))
                dve.wait_ge(carry_T, t + 1)
                v.tensor_scalar(pmax[:, 1, :], pB[:, P:P + SW], flags[:, 0:1], None, ALU.add)
                dve.drain()
                v.tensor_tensor(pmax[:, 2, :], pmax[:, 0, :], pmax[:, 1, :], ALU.max)
                dve.drain()
                v.tensor_tensor(pexp[:, 0, :], pmax[:, 0, :], pmax[:, 2, :], ALU.subtract)
                v.tensor_tensor(pexp[:, 1, :], pmax[:, 1, :], pmax[:, 2, :], ALU.subtract).then_inc(tail_in, 1)
                dve.wait_ge(tail_exp, 2 * t + 2)
                v.tensor_tensor(pexp[:, 0, :], pexp[:, 0, :], patch[:, 0:SW], ALU.mult)
                v.tensor_tensor(pexp[:, 1, :], pexp[:, 1, :], pB[:, 0:SW], ALU.mult)
                dve.drain()
                v.tensor_tensor(patch[:, 0:SW], pexp[:, 0, :], pexp[:, 1, :], ALU.add).then_inc(patch_ready, 1)

            def put_ids(g, k):
                v.tensor_copy(end_ring[:, k, :], end_ids[:, bass.ds(g * GN, GN)]).then_inc(node_ids, 1)

            def node_means(t, it, k, q):
                g = 2 * it + k
                dve.drain()
                dve.wait_ge(nodes_fetched[k], 16 * GN * (t * PAIRS + it + 1))
                r = node4[k][:, :, 0:SW].rearrange("p n (h c) -> p n h c", h=H)
                v.reciprocal(rden[:, :, :], r[:, :, :, CH])
                dve.drain()
                v.tensor_tensor(rden[:, :, :], rden[:, :, :],
                                has[:, bass.ds(g * GN, GN)][:, :, None].to_broadcast([P, GN, H]), ALU.mult)
                dve.drain()
                if q is not None:
                    dve.wait_ge(h_T, q + 1)
                    dve.sem_inc(dve_turn, 1)
                v.tensor_tensor(hg2[:, :, :].rearrange("p n (h c) -> p n h c", h=H), r[:, :, :, 0:CH],
                                rden[:, :, :, None].to_broadcast([P, GN, H, CH]), ALU.mult)
                dve.drain()
                put_ids(g + 2, k)

            def layer_norm(g, i, target):
                mine = feats[:, bass.ds(g * GN, GN), :]
                v.tensor_tensor(hg2[:, :, :], hg2[:, :, :], mine, ALU.add)
                dve.drain()
                v.tensor_reduce(mean[:, :], hg2[:, :, :], AX, ALU.add)
                dve.drain()
                v.tensor_scalar(mean[:, :], mean[:, :], 1.0 / C, None, ALU.mult)
                dve.drain()
                v.tensor_tensor(hg2[:, :, :], hg2[:, :, :], mean[:, :, None].to_broadcast([P, GN, C]), ALU.subtract)
                dve.drain()
                v.tensor_tensor(sq[:, :, :], hg2[:, :, :], hg2[:, :, :], ALU.mult)
                dve.drain()
                v.tensor_reduce(var[:, :], sq[:, :, :], AX, ALU.add)
                dve.drain()
                v.tensor_scalar(var[:, :], var[:, :], 1.0 / C, LN_EPS, ALU.mult, ALU.add).then_inc(var_ready, 1)
                dve.wait_ge(dev_ready, i + 2)
                v.reciprocal(var[:, :], var[:, :])
                dve.drain()
                return v.tensor_tensor(target if target is not None else mine, hg2[:, :, :],
                                       var[:, :, None].to_broadcast([P, GN, C]), ALU.mult)

            def gat_pass(L):
                with dve.Fori(0, ITER) as it:
                    dve.drain()
                    dve.wait_ge(alpha_loaded, 16 * (L * ITER + it + 1))
                    v.tensor_copy(alpha_e[:, :, 0:1], alpha_e[:, :, JI:JI + 1])
                    dve.drain()
                    for h in range(H):
                        last = v.tensor_tensor_scan(alpha_e[:, h, 1:JI + 1], keep[:, bass.ds(it * JI, JI)],
                                                    alpha_raw[:, :, h], alpha_e[:, h, 0:1], ALU.mult, ALU.add)
                    last.then_inc(alpha_free, 1)
                    dve.drain()
                    for b in range(SLOTS):
                        K = L * CHUNKS + it * SLOTS + b
                        dve.wait_ge(gat_gathered[b], ONE_STEP * (L * ITER + it + 1))
                        v.tensor_tensor(logit0[:, :, :], slot_rows[:, b, :, C:C + 2].rearrange("p j h -> p h j"),
                                        alpha_e[:, :, 1 + b * J:1 + (b + 1) * J], ALU.add)
                        dve.drain()
                        v.scalar_tensor_tensor(logit[:, :, :], logit0[:, :, :], SLOPE1, logit0[:, :, :], ALU.mult, ALU.max)
                        dve.wait_ge(rows_staged, CHUNKS + K + 2)
                        dve.sem_inc(dve_turn, 1)
                        v.tensor_copy(run_max[:, :, 0:1], run_max[:, :, J:J1])
                        v.tensor_copy(X3[:, :, 0:1], S3[:, :, J:J1])
                        dve.drain()
                        mask = reset[:, bass.ds(it * JI + b * J, J)]
                        for h in range(H):
                            v.tensor_tensor_scan(run_max[:, h, 1:J1], mask, logit[:, h, :], run_max[:, h, 0:1],
                                                 ALU.add, ALU.max)
                        dve.drain()
                        v.tensor_tensor(exps[:, 0, :, :], run_max[:, :, 0:J],
                                        mask[:, None, :].to_broadcast([P, H, J]), ALU.add)
                        v.tensor_tensor(exps[:, 1, :, :], logit[:, :, :], run_max[:, :, 1:J1], ALU.subtract)
                        dve.drain()
                        v.tensor_tensor(exps[:, 0, :, :], exps[:, 0, :, :], run_max[:, :, 1:J1], ALU.subtract)\
                            .then_inc(exps_in, 1)
                        dve.wait_ge(weights_ready, K + 1)
                        v.tensor_tensor(X4[:, :, 0:CH, 1:J1],
                                        slot_rows[:, b, :, 0:C].rearrange("p j (h c) -> p h c j", h=H),
                                        X4[:, :, CH:CH + 1, 1:J1].to_broadcast([P, H, CH, J]), ALU.mult)
                        dve.drain()
                        v.tensor_tensor_scan(S[:, :], F[:, :], X[:, :], 0.0, ALU.mult, ALU.add).then_inc(gat_sum, 1)
                        v.tensor_copy(ring_ids[:, b * J:(b + 1) * J], src_ids[:, bass.ds((it + 1) * JI + b * J, J)])\
                            .then_inc(slot_ready, 1)
                dve.drain()
                dve.wait_ge(rows_staged, (L + 2) * CHUNKS + 2)
                dve.sem_inc(dve_turn, 1)

            def node_groups(t, finish):
                dve.drain()
                for k in range(2):
                    put_ids(k, k)
                with dve.Fori(0, PAIRS) as it:
                    for k in range(2):
                        finish(it, k)

            def after_conv(it, k):
                q = GROUPS + 2 * it + k
                node_means(0, it, k, q)
                v.tensor_tensor(hg2[:, :, :], hg2[:, :, :], bn_s[:, None, :].to_broadcast([P, GN, C]), ALU.mult)
                dve.drain()
                layer_norm(2 * it + k, 2 * it + k, hg[:, :, :])
                dve.drain()
                v.tensor_copy(feats[:, bass.ds((2 * it + k) * GN, GN), :], hg[:, :, :]).then_inc(h_ready, 1)

            complete_first_rows(0)
            v.tensor_copy(wl[:, :], wcat[:, 0, :])
            node_groups(0, after_conv)
            gat_pass(0)

            with dve.Fori(1, LAYERS) as L:
                complete_first_rows(L)
                v.tensor_copy(wl[:, :], wcat[:, bass.ds(L, 1), :].rearrange("k a r -> k (a r)"))
                dve.drain()
                v.tensor_copy(bias_l[:, :], biasb[:, bass.ds(L - 1, 1), :].rearrange("p a c -> p (a c)"))

                def after_gat(it, k):
                    q = (L + 1) * GROUPS + 2 * it + k
                    node_means(L, it, k, q)
                    v.tensor_tensor(hg2[:, :, :], hg2[:, :, :], bias_l[:, None, :].to_broadcast([P, GN, C]), ALU.add)
                    dve.drain()
                    v.tensor_scalar(hg[:, :, :], hg2[:, :, :], 0.0, None, ALU.max).then_inc(h_ready, 1)

                node_groups(L, after_gat)
                gat_pass(L)

            complete_first_rows(LAYERS)

            def after_last(it, k):
                node_means(LAYERS, it, k, None)
                v.tensor_tensor(hg2[:, :, :], hg2[:, :, :], biasb[:, LAYERS - 1, None, :].to_broadcast([P, GN, C]), ALU.add)
                dve.drain()
                layer_norm(2 * it + k, GROUPS + 2 * it + k, None).then_inc(out_ready, 1)

            node_groups(LAYERS, after_last)


_WEIGHTS = ["L1_gnn_Ws", "L1_gnn_Wd", "L1_gnn_as", "L1_gnn_ad", "L1_gnn_b"]


def kernel(**inputs):
    import concourse.bacc as bacc
    from concourse.bass_utils import run_bass_kernel_spmd as run

    nc = bacc.Bacc("TRN2", target_bir_lowering=False, num_devices=1)
    arrays = {}

    def given(name):
        a = np.ascontiguousarray(inputs[name])
        arrays[name] = a
        return nc.dram_tensor(name, a.shape, mybir.dt.from_np(a.dtype), kind="ExternalInput").ap()

    first = [given(n) for n in ("x", "src", "dst", "L0_gnn_W", "L0_gnn_b", "L0_gnn_gamma", "L0_gnn_beta")]
    layers = [[given(f"{n}{l + 1}") for l in range(LAYERS)] for n in _WEIGHTS]
    out = nc.dram_tensor("out", (N, C), mybir.dt.float32, kind="ExternalOutput").ap()
    build(nc, *first, *layers, out)
    return run(nc, [arrays], core_ids=[0]).results[0]["out"]
```

```python
from contextlib import ExitStack

import numpy as np

import concourse.bass as bass
from concourse import mybir

P = 128
N, E, C, H, CH = 12500, 400000, 64, 2, 32
EPP = E // P
J = 25
SLOTS = 5
ITER = EPP // (J * SLOTS)
JI = J * SLOTS
CHUNKS = EPP // J
NPP = 98
NPAD = NPP * P
LASTN = N - (P - 1) * NPP
GN = 7
GROUPS = NPP // GN
PAIRS = GROUPS // 2
ROW = C + 4
SW = H * (CH + 1)
J1 = J + 1
QB, QS = 11, 3
QN = QB * QS
BL = 125
BPP = EPP // BL
LAYERS = 3
BIG = 3.0e38
TINY = 1.0e-30
BN_EPS, LN_EPS = 1e-5, 1e-5
SLOPE0, SLOPE1 = 0.3, 0.2
ONE_STEP = J * 16


def build(nc, x, src, dst, W0, b0, gamma, beta, Ws, Wd, a_s, a_d, bias, out):
    f32, i32, bf16 = mybir.dt.float32, mybir.dt.int32, mybir.dt.bfloat16
    ALU, ACT, AX = mybir.AluOpType, mybir.ActivationFunctionType, mybir.AxisListType.X
    ctx = ExitStack()
    with ctx:
        def sb(name, shape, dt=f32):
            return ctx.enter_context(nc.sbuf_tensor(name, shape, dt))

        def ps(name, shape):
            return ctx.enter_context(nc.psum_tensor(name, shape, f32))

        def sem(name):
            return ctx.enter_context(nc.semaphore(name))

        def dram(name, shape, dt=f32):
            return nc.dram_tensor(name, shape, dt, kind="Internal").ap()

        table = dram("table", (NPAD, ROW))
        dst_term = dram("dst_term", (NPAD, C))
        sums = dram("sums", (E, ROW))
        conv_dst = dram("conv_dst", (E + NPAD, C))
        gat_dst = dram("gat_dst", (E + NPAD, 2))
        msgs = dram("msgs", (CHUNKS, P, C * J))

        src_ids = sb("src_ids", [P, EPP + JI], i32)
        keep = sb("keep", [P, EPP])
        reset = sb("reset", [P, EPP])
        feats_pad = sb("feats_pad", [P, (NPP + GN) * C])
        rows = sb("rows", [P, SLOTS * J * ROW])
        ring_ids = sb("ring_ids", [P, JI], i32)
        X = sb("X", [P, SW * J1])
        F = sb("F", [P, SW * J1])
        S = sb("S", [P, SW * J1])
        stage_rows = sb("stage_rows", [P, J, ROW])
        ein = sb("ein", [P, C * J])
        z = sb("z", [P, C * J])
        z2 = sb("z2", [P, C * J])
        run_max = sb("run_max", [P, H, J1])
        logit0 = sb("logit0", [P, H, J])
        logit = sb("logit", [P, H, J])
        exps = sb("exps", [P, 2, H, J])
        alpha_raw = sb("alpha_raw", [P, JI, 2])
        alpha_e = sb("alpha_e", [P, H, JI + 1])
        node_rows = sb("node_rows", [P, 2, GN * ROW])
        feats = feats_pad[:, 0:NPP * C].rearrange("p (n c) -> p n c", c=C)
        hg = sb("hg", [P, GN, C])
        hg2 = sb("hg2", [P, GN, C])
        rden = sb("rden", [P, GN, H])
        mean = sb("mean", [P, GN])
        var = sb("var", [P, GN])
        hT = sb("hT", [C, GN * P])
        tstage = sb("tstage", [P, 2, GN * ROW])
        astage = sb("astage", [P, 2, GN * C])
        end_ids = sb("end_ids", [P, NPP + 2 * GN], i32)
        start_ids = sb("start_ids", [P, NPP], i32)
        end_ring = sb("end_ring", [P, 2, GN], i32)
        start_ring = sb("start_ring", [P, 2, GN], i32)
        has = sb("has", [P, NPP])
        first_ids = sb("first_ids", [P, 1], i32)
        patch_ids = sb("patch_ids", [P, 1], i32)
        first_rows = sb("first_rows", [P, ROW])
        ident = sb("ident", [P, P])
        ones = sb("ones", [P, P])
        w0 = sb("w0", [C, 2 * C])
        rhs0 = sb("rhs0", [C, ROW + C])
        ws = sb("ws", [C, LAYERS, C])
        wd = sb("wd", [C, LAYERS, C])
        asb = sb("asb", [C, LAYERS, C])
        adb = sb("adb", [C, LAYERS, C])
        wcat = sb("wcat", [C, LAYERS, ROW])
        wl = sb("wl", [C, ROW])
        biasb = sb("biasb", [P, LAYERS, C])
        b0b = sb("b0b", [P, C])
        gammab = sb("gammab", [P, C])
        betab = sb("betab", [P, C])
        stat = sb("stat", [P, 2, C])
        part = sb("part", [P, 2, C])
        bn = sb("bn", [P, 2, C])
        bn_s = sb("bn_s", [P, C])
        bn_t = sb("bn_t", [P, C])
        prev_i = sb("prev_i", [P, 1], i32)
        flags = sb("flags", [P, 6])
        edge0 = sb("edge0", [P, 1], i32)
        sign = sb("sign", [P, C])
        places = sb("places", [P, NPP])
        tmp_end, tmp_none, tmp_start = (sb(n, [P, NPP]) for n in ("tmp_end", "tmp_none", "tmp_start"))
        sq = sb("sq", [P, GN, C])
        bias_l = sb("bias_l", [P, C])
        tri = sb("tri", [P, P])
        steps = sb("steps", [P, P])
        before = sb("before", [P, 1])
        hist = sb("hist", [P, NPP + 1])
        query = sb("query", [P, NPP + 1 + QN])
        count = sb("count", [P, NPP + 1])
        qi = sb("qi", [P, NPP + 1 + QN], i32)
        blk = sb("blk", [P, NPP + 1 + QN])
        cnt = sb("cnt", [P, QB])
        blk_i = sb("blk_i", [P, QN], i32)
        step_i = sb("step_i", [P, P], i32)
        owner, within = sb("owner", [P, BPP]), sb("within", [P, BPP])
        reset_row = sb("reset_row", [SW, P])
        ends = sb("ends", [P, 2, SW])
        max_row = sb("max_row", [SW, P + 1])
        sum_row = sb("sum_row", [SW, P + 1])
        tail_row = sb("tail_row", [SW, 2, P])
        patch = sb("patch", [P, ROW])
        pmax = sb("pmax", [P, 3, SW])
        pexp = sb("pexp", [P, 2, SW])

        dst_i = rows[:, 0:EPP].bitcast(i32)
        D = rows[:, EPP:2 * EPP]
        got = [rows[:, a:a + QB * BL].bitcast(i32).rearrange("p (q k) -> p q k", k=BL)
               for a in (0, QB * BL, 2 * EPP)]
        got_f = X[:, 0:QB * BL].rearrange("p (q k) -> p q k", k=BL)
        cmp_b = ein[:, 0:QB * BL].rearrange("p (q k) -> p q k", k=BL)
        hot_p = F[:, :].bitcast(bf16)[:, 0:BPP * P].rearrange("p (t q) -> p t q", q=P)
        hot_i = S[:, :].bitcast(bf16)[:, 0:BPP * NPP].rearrange("p (t i) -> p t i", i=NPP)
        wide = ein[:, :], X[:, :]

        slot_rows = rows[:, :].rearrange("p (s j r) -> p s j r", s=SLOTS, r=ROW)
        CW = SW * J1
        X2, F2, S2 = (rows[:, n * CW:(n + 1) * CW] for n in range(3))
        stage2 = rows[:, 3 * CW:3 * CW + J * ROW].rearrange("p (j r) -> p j r", r=ROW)
        in2 = rows[:, 3 * CW + J * ROW:3 * CW + J * ROW + C * J]
        conv_in, conv_u = (ein[:, :], in2), (z[:, :], z2[:, :])
        conv_x, conv_f, conv_s = (X[:, :], X2), (F[:, :], F2), (S[:, :], S2)
        conv_st = (stage_rows[:, :, :], stage2)

        X4 = X[:, :].rearrange("p (h c j) -> p h c j", h=H, j=J1)
        F4 = F[:, :].rearrange("p (h c j) -> p h c j", h=H, j=J1)
        S3 = S[:, :].rearrange("p (c j) -> p c j", j=J1)
        X3 = X[:, :].rearrange("p (c j) -> p c j", j=J1)
        F3 = F[:, :].rearrange("p (c j) -> p c j", j=J1)
        z3 = z[:, :].rearrange("p (c j) -> p c j", j=J)
        z23 = z2[:, :].rearrange("p (c j) -> p c j", j=J)
        ein_jc = ein[:, :].rearrange("p (j c) -> p j c", c=C)
        node4 = [node_rows[:, k, :].rearrange("p (n r) -> p n r", r=ROW) for k in range(2)]
        tst = [tstage[:, k, :].rearrange("p (n r) -> p n r", r=ROW) for k in range(2)]
        ast = [astage[:, k, :].rearrange("p (n r) -> p n r", r=C) for k in range(2)]

        pT = ps("pT", [P, 2, 512])
        pP = ps("pP", [P, 3, 512])
        conv_p6 = pP[:, 0:2, 0:3 * (ROW + C)].rearrange("p m (n r) -> p m n r", n=3)
        pR = ps("pR", [P, 512])
        pB = ps("pB", [P, 512])
        pS = ps("pS", [P, 512])

        in_dst, in_prev, in_src, in_x, in_w0, in_w = (
            sem(n) for n in ("in_dst", "in_prev", "in_src", "in_x", "in_w0", "in_w"))
        zero_filled = [sem(f"zero_filled{k}") for k in range(2)]
        gat_zeroed = sem("gat_zeroed")
        searched = [sem(f"searched{k}") for k in range(QS)]
        table_written = [sem(f"table_written{k}") for k in range(2)]
        starts_scattered = [sem(f"starts_scattered{k}") for k in range(2)]
        firsts_gathered, firsts_written = sem("firsts_gathered"), sem("firsts_written")
        conv_gathered = [sem(f"conv_gathered{k}") for k in range(SLOTS)]
        gat_gathered = [sem(f"gat_gathered{k}") for k in range(SLOTS)]
        ein_loaded, msgs_stored = sem("ein_loaded"), sem("msgs_stored")
        sums_stored = [sem(f"sums_stored{k}") for k in range(2)]
        msgs_loaded = [sem(f"msgs_loaded{k}") for k in range(2)]
        terms_loaded = [sem(f"terms_loaded{k}") for k in range(2)]
        terms_scattered = [sem(f"terms_scattered{k}") for k in range(2)]
        alpha_loaded = sem("alpha_loaded")
        nodes_fetched = [sem(f"nodes_fetched{k}") for k in range(2)]
        patch_gathered, patch_scattered = sem("patch_gathered"), sem("patch_scattered")
        out_stored = sem("out_stored")
        zeros_ready, consts_ready, clears_done, conv_ready = (
            sem(n) for n in ("zeros_ready", "consts_ready", "clears_done", "conv_ready"))
        w0_T, w0_ready = sem("w0_T"), sem("w0_ready")
        hot_ready, hist_ready, totals_ready, before_ready = (
            sem(n) for n in ("hot_ready", "hist_ready", "totals_ready", "before_ready"))
        search_ready, ids_ready = sem("search_ready"), sem("ids_ready")
        flag_ready, flag_T = sem("flag_ready"), sem("flag_T")
        pool_turn = sem("pool_turn")
        sp_turn, act_turn, pe_turn, dve_turn = (sem(n) for n in ("sp_turn", "act_turn", "pe_turn", "dve_turn"))
        h_ready, h_T, hT_ready, projected, staged = (
            sem(n) for n in ("h_ready", "h_T", "hT_ready", "projected", "staged"))
        stage_free = [sem(f"stage_free{k}") for k in range(2)]
        slot_ready = sem("slot_ready")
        ein_free, X_ready, X_free, z_ready, z_free = (
            sem(n) for n in ("ein_free", "X_ready", "X_free", "z_ready", "z_free"))
        stat_ready, stat_summed = sem("stat_ready"), sem("stat_summed")
        var_ready, dev_ready = sem("var_ready"), sem("dev_ready")
        bn_ready, shifted, conv_u_free, conv_F, conv_sum, starts_ready, search_done = (
            sem(n) for n in ("bn_ready", "shifted", "conv_u_free", "conv_F", "conv_sum", "starts_ready",
                            "search_done"))
        rows_staged, sums_free = sem("rows_staged"), sem("sums_free")
        alpha_free = sem("alpha_free")
        exps_in, weights_ready, gat_sum = sem("exps_in"), sem("weights_ready"), sem("gat_sum")
        node_ids = sem("node_ids")
        ends_ready, ends_T, tail_in, tail_exp, carry_ready, carry_T, patch_ready = (
            sem(n) for n in ("ends_ready", "ends_T", "tail_in", "tail_exp", "carry_ready", "carry_T", "patch_ready"))
        out_ready = sem("out_ready")

        x_p = x[0:(P - 1) * NPP, :].rearrange("(p i) c -> p i c", i=NPP)
        out_p = out[0:(P - 1) * NPP, :].rearrange("(p i) c -> p i c", i=NPP)
        PARTS = ((0, 112), (112, P - 1))
        table_p = table.rearrange("(p i) r -> p i r", i=NPP)
        dterm_p = dst_term.rearrange("(p i) r -> p i r", i=NPP)
        sums_p = sums.rearrange("(p j) r -> p j r", j=EPP)
        convd_p = conv_dst[0:E, :].rearrange("(p j) r -> p (j r)", j=EPP)
        gatd_p = gat_dst[0:E, :].rearrange("(p j) r -> p j r", j=EPP)
        dst_p = dst.rearrange("(p j) -> p j", j=EPP)
        dst_blocks = dst.rearrange("(b k) -> b k", k=BL)

        block = ctx.enter_context(nc.Block())

        @block.sync
        def _(sp):
            def held(s, v):
                sp.wait_ge(s, v)
                sp.sem_inc(sp_turn, 1)

            sp.dma_start(dst_i, dst_p).then_inc(in_dst, 16)
            sp.wait_ge(clears_done, 1)
            with nc.allow_non_contiguous_dma(reason="one id per partition"):
                sp.dma_start(prev_i[1:P, :], dst_p[0:P - 1, EPP - 1:EPP]).then_inc(in_prev, 16)
            for lo, hi in PARTS:
                sp.dma_start(feats[lo:hi, :, :], x_p[lo:hi, :, :]).then_inc(in_x, 16)
            sp.dma_start(feats[P - 1:P, 0:LASTN, :], x[(P - 1) * NPP:N, :].rearrange("(a i) c -> a i c", a=1)).then_inc(in_x, 16)
            sp.dma_start(w0[:, :], W0).then_inc(in_w0, 16)
            for t, v in ((b0b, b0), (gammab, gamma), (betab, beta)):
                sp.dma_start(t[:, :], v.partition_broadcast(P)).then_inc(in_w0, 16)
            sp.dma_start(src_ids[:, 0:EPP], src.rearrange("(p j) -> p j", j=EPP)).then_inc(in_src, 16)
            sp.dma_start(src_ids[:, EPP:EPP + JI], src.rearrange("(p j) -> p j", j=EPP)[:, 0:JI]).then_inc(in_src, 16)
            for l in range(LAYERS):
                sp.dma_start(ws[:, l, :], Ws[l]).then_inc(in_w, 16)
                sp.dma_start(wd[:, l, :], Wd[l]).then_inc(in_w, 16)
                sp.dma_start(asb[:, l, :], a_s[l].rearrange("h c -> (h c)").partition_broadcast(C)).then_inc(in_w, 16)
                sp.dma_start(adb[:, l, :], a_d[l].rearrange("h c -> (h c)").partition_broadcast(C)).then_inc(in_w, 16)
                sp.dma_start(biasb[:, l, :], bias[l].partition_broadcast(P)).then_inc(in_w, 16)
            for k in range(2):
                sp.sem_inc(stage_free[k], 1)
            sp.sem_inc(z_free, 1)
            sp.sem_inc(sums_free, 2)
            sp.sem_inc(alpha_free, 1)

            EARLY, PER_PAIR = 2, 2

            def zero_fill(n, k):
                sp.dma_start(convd_p[:, bass.ds(n * (JI * C), JI * C)].rearrange("p (a n) -> p a n", a=SLOTS),
                             z[:, None, :].to_broadcast([P, SLOTS, J * C])).then_inc(zero_filled[k], 16)

            sp.wait_ge(zeros_ready, 1)
            sp.dma_start(gatd_p[:, :, :].rearrange("p (a j) r -> p a (j r)", a=5),
                         z[:, None, 0:EPP * 2 // 5].to_broadcast([P, 5, EPP * 2 // 5])).then_inc(gat_zeroed, 16)
            for n in range(EARLY):
                zero_fill(n, n % 2)

            def write_table(stage, h0):
                with sp.Fori(0, PAIRS) as it:
                    for k in range(2):
                        held(staged, 2 * (h0 + it) + k + 2)
                        sp.dma_start(table_p[:, bass.ds((2 * it + k) * GN, GN), :], tst[k]).then_inc(table_written[k], 16)
                        if stage == 0:
                            sp.dma_start(dterm_p[:, bass.ds((2 * it + k) * GN, GN), :], ast[k]).then_inc(table_written[k], 16)
                    if stage == 0:
                        for n in range(PER_PAIR):
                            zero_fill(it * PER_PAIR + EARLY + n, n % 2)
                    for k in range(2):
                        done = h0 + it + 1
                        held(table_written[k], 32 * (it + 1) if stage == 0 else 16 * (done + PAIRS))
                        if stage > 0:
                            held(starts_scattered[k], 16 * GN * (done - PAIRS))
                        sp.sem_inc(stage_free[k], 1)

            write_table(0, 0)
            FILLED = EARLY + PER_PAIR * PAIRS
            with sp.Fori(0, (ITER - FILLED) // 2) as it:
                for k in range(2):
                    held(zero_filled[k], 16 * (it + FILLED // 2))
                    zero_fill(2 * it + FILLED + k, k)
            zero_fill(ITER - 1, 0)

            def load_terms(it, k):
                sp.dma_start(ast[k], dterm_p[:, bass.ds((2 * it + k) * GN, GN), :]).then_inc(terms_loaded[k], 16)

            for k in range(2):
                load_terms(0, k)
            with sp.Fori(1, PAIRS) as it:
                for k in range(2):
                    held(terms_scattered[k], 16 * GN * it)
                    load_terms(it, k)
            sp.wait_ge(firsts_gathered, 16)
            for k in range(2):
                sp.wait_ge(terms_scattered[k], 16 * GN * PAIRS)
            sp.dma_start(convd_p[:, 0:C], first_rows[:, 0:C]).then_inc(firsts_written, 16)
            sp.wait_ge(firsts_written, 16)

            with sp.Fori(0, CHUNKS) as c:
                held(ein_free, c + 1)
                sp.dma_start(ein[:, :], convd_p[:, bass.ds(c * (J * C), J * C)]).then_inc(ein_loaded, 16)
                held(z_ready, c + 1)
                sp.dma_start(msgs[bass.ds(c, 1), :, :].rearrange("a p n -> (a p) n"), z[:, :]).then_inc(msgs_stored, 16)
                held(msgs_stored, 16 * (c + 1))
                sp.sem_inc(z_free, 1)

            def load_msgs(c, k):
                sp.dma_start(conv_in[k], msgs[bass.ds(c, 1), :, :].rearrange("a p n -> (a p) n")).then_inc(msgs_loaded[k], 16)

            def store_sums(K, row0, k):
                held(rows_staged, K + 3)
                sp.dma_start(sums_p[:, bass.ds(row0, J), :], conv_st[k]).then_inc(sums_stored[k], 16)

            def sums_are_stored(k, uses):
                held(sums_stored[k], 16 * uses)
                sp.sem_inc(sums_free, 1)

            def conv_step(c, k, more):
                if more:
                    held(shifted, c + 1)
                    load_msgs(c + 2, k)
                store_sums(c, c * J, k)

            load_msgs(0, 0)
            sp.wait_ge(conv_ready, 1)
            load_msgs(1, 1)
            conv_step(0, 0, True)
            with sp.Fori(0, CHUNKS // 2 - 1) as it:
                conv_step(2 * it + 1, 1, True)
                sums_are_stored(0, it + 1)
                conv_step(2 * it + 2, 0, True)
                sums_are_stored(1, it + 1)
            conv_step(CHUNKS - 2, 1, False)
            sums_are_stored(0, CHUNKS // 2)
            conv_step(CHUNKS - 1, 0, False)
            sums_are_stored(1, CHUNKS // 2)
            sums_are_stored(0, CHUNKS // 2 + 1)

            def gat_layer(L):
                write_table(1, (L + 1) * PAIRS)
                held(firsts_gathered, 16 * (L + 2))
                with nc.allow_non_contiguous_dma(reason="two values per partition"):
                    sp.dma_start(gatd_p[:, 0:1, :].rearrange("p a r -> p (a r)"), first_rows[:, C + 2:ROW]).then_inc(firsts_written, 16)
                held(firsts_written, 16 * (L + 2))
                with sp.Fori(0, ITER) as it:
                    held(alpha_free, L * ITER + it + 1)
                    sp.dma_start(alpha_raw[:, :, :], gatd_p[:, bass.ds(it * JI, JI), :]).then_inc(alpha_loaded, 16)
                    for b in range(SLOTS):
                        K = (L + 1) * CHUNKS + it * SLOTS + b
                        store_sums(K, it * JI + b * J, 0)
                        sums_are_stored(0, K + 1 - CHUNKS // 2)

            with sp.Fori(0, LAYERS) as L:
                gat_layer(L)

            half = NPP // 2
            for n, (a, b) in enumerate(((0, half), (half, NPP))):
                sp.wait_ge(out_ready, (n + 1) * GROUPS // 2)
                for lo, hi in PARTS:
                    sp.dma_start(out_p[lo:hi, a:b, :], feats[lo:hi, a:b, :]).then_inc(out_stored, 16)
                e = min(b, LASTN)
                sp.dma_start(out[(P - 1) * NPP + a:(P - 1) * NPP + e, :].rearrange("(a i) c -> a i c", a=1),
                             feats[P - 1:P, a:e, :]).then_inc(out_stored, 16)
            sp.wait_ge(out_stored, 96)

        @block.gpsimd
        def _(pool):
            def at(col):
                return bass.IndirectOffsetOnAxis(ap=col, axis=0)

            def gather(out_, table_, col):
                return pool.indirect_dma_start(out=out_, out_offset=None, in_=table_, in_offset=at(col))

            def scatter(table_, col, in_):
                return pool.indirect_dma_start(out=table_, out_offset=at(col), in_=in_, in_offset=None)

            pool.memset(ident[:, :], 0.0)
            pool.iota(qi[:, :], pattern=[[1, NPP + 1 + QN]], base=-1, channel_multiplier=NPP)
            pool.memset(tri[:, :], 1.0)
            pool.iota(step_i[:, :], pattern=[[NPP, P]], base=0, channel_multiplier=0)
            pool.iota(edge0[:, :], pattern=[[1, 1]], base=0, channel_multiplier=EPP)
            pool.drain()
            pool.affine_select(out=ident[:, :], in_=ident[:, :], compare_op=ALU.not_equal, fill=1.0, base=0,
                               pattern=[[-1, P]], channel_multiplier=1)
            pool.affine_select(out=tri[:, :], in_=tri[:, :], compare_op=ALU.is_gt, fill=0.0, base=0,
                               pattern=[[1, P]], channel_multiplier=-1).then_inc(consts_ready, 1)

            with pool.Fori(0, (NPP + 1) // QN) as it:
                for k in range(QS):
                    pool.wait_ge(search_ready, it * QS + k + 1)
                    pool.sem_inc(pool_turn, 1)
                    for q in range(QB):
                        gather(got[k][:, q, :], dst_blocks, blk_i[:, k * QB + q:k * QB + q + 1]).then_inc(searched[k], 16)

            def scatter_starts(k, target, values, scattered):
                for n in range(GN):
                    scatter(target, start_ring[:, k, n:n + 1], values[:, n, :]).then_inc(scattered[k], 16)

            def table_done(uses):
                for k in range(2):
                    pool.wait_ge(stage_free[k], uses + 1)
                pool.sem_inc(pool_turn, 1)

            def gather_firsts(source, width):
                gather(first_rows[:, 0:width], source, first_ids[:, 0:1]).then_inc(firsts_gathered, 16)

            def edge_turn(gathered, K0, it):
                for b in range(SLOTS):
                    pool.wait_ge(slot_ready, K0 + it * SLOTS + b + 1)
                    pool.sem_inc(pool_turn, 1)
                    for j in range(J):
                        gather(slot_rows[:, b, j, :], table, ring_ids[:, b * J + j:b * J + j + 1])\
                            .then_inc(gathered[b], 16)

            def complete_first_rows(t):
                pool.wait_ge(sums_free, (t + 1) * CHUNKS + 2)
                pool.sem_inc(pool_turn, 1)
                gather(patch[:, :], sums, patch_ids[:, 0:1]).then_inc(patch_gathered, 16)
                pool.wait_ge(patch_ready, t + 1)
                pool.sem_inc(pool_turn, 1)
                scatter(sums, patch_ids[:, 0:1], patch[:, :]).then_inc(patch_scattered, 16)
                pool.wait_ge(patch_scattered, 16 * (t + 1))
                pool.sem_inc(pool_turn, 1)

            def fetch_nodes(t, it, k):
                pool.wait_ge(node_ids, t * (GROUPS + 2) + 2 * it + k + 1)
                pool.sem_inc(pool_turn, 1)
                for n in range(GN):
                    gather(node4[k][:, n, :], sums, end_ring[:, k, n:n + 1]).then_inc(nodes_fetched[k], 16)

            table_done(PAIRS)
            pool.wait_ge(search_done, 1)
            gather_firsts(dst_term, C)
            edge_turn(conv_gathered, 0, 0)
            pool.wait_ge(zero_filled[0], 16 * (ITER // 2 + 1))
            pool.wait_ge(zero_filled[1], 16 * (ITER // 2))
            pool.wait_ge(gat_zeroed, 16)
            pool.sem_inc(pool_turn, 1)
            with pool.Fori(0, PAIRS) as it:
                for k in range(2):
                    pool.wait_ge(terms_loaded[k], 16 * (it + 1))
                    pool.sem_inc(pool_turn, 1)
                    pool.wait_ge(starts_ready, 2 * it + k + 1)
                    pool.sem_inc(pool_turn, 1)
                    scatter_starts(k, conv_dst, ast[k], terms_scattered)
            with pool.Fori(1, ITER) as it:
                edge_turn(conv_gathered, 0, it)

            def shift(c, k, n):
                pool.wait_ge(msgs_loaded[k], 16 * (n + 1))
                pool.sem_inc(pool_turn, 1)
                pool.wait_ge(conv_u_free, c + 1)
                pool.tensor_tensor(conv_u[k].rearrange("p (c j) -> p c j", j=J),
                                   conv_in[k].rearrange("p (c j) -> p c j", j=J),
                                   bn_t[:, :, None].to_broadcast([P, C, J]), ALU.add).then_inc(shifted, 1)

            pool.wait_ge(conv_ready, 1)
            with pool.Fori(0, CHUNKS // 2) as it:
                for k in range(2):
                    shift(2 * it + k, k, it)
            shift(CHUNKS - 1, 0, CHUNKS // 2)

            with pool.Fori(0, LAYERS) as L:
                complete_first_rows(L)
                def scatter_alphas(it, k):
                    pool.wait_ge(staged, (L + 1) * GROUPS + 2 * it + k + 2)
                    pool.sem_inc(pool_turn, 1)
                    scatter_starts(k, gat_dst, tst[k][:, :, C + 2:ROW], starts_scattered)

                for k in range(2):
                    fetch_nodes(L, 0, k)
                with pool.Fori(0, PAIRS - 1) as it:
                    for k in range(2):
                        fetch_nodes(L, it + 1, k)
                        scatter_alphas(it, k)
                for k in range(2):
                    scatter_alphas(PAIRS - 1, k)
                table_done((L + 2) * PAIRS)
                gather_firsts(table, ROW)
                with pool.Fori(0, ITER) as it:
                    edge_turn(gat_gathered, (L + 1) * CHUNKS, it)
            complete_first_rows(LAYERS)
            with pool.Fori(0, PAIRS) as it:
                for k in range(2):
                    fetch_nodes(LAYERS, it, k)

        @block.scalar
        def _(act):
            def held(s, v):
                act.wait_ge(s, v)
                act.sem_inc(act_turn, 1)

            act.sem_inc(staged, 1)
            act.sem_inc(ein_free, 1)
            act.sem_inc(rows_staged, 2)
            act.wait_ge(in_x, 48)

            def project(stage, h0):
                with act.Fori(0, PAIRS) as it:
                    for k in range(2):
                        q = 2 * (h0 + it) + k
                        if stage == 1:
                            deviation(2 * it + k)
                        act.wait_ge(h_T, q + 2)
                        nc.scalar.copy(hT[:, 0:4 * P], pT[0:C, 0, 0:4 * P])
                        nc.scalar.copy(hT[:, 4 * P:GN * P], pT[0:C, 1, 0:3 * P]).then_inc(hT_ready, 1)
                        if stage == 0:
                            nc.scalar.copy(hg[:, :, :], feats_pad[:, bass.ds((q + 1) * GN * C, GN * C)]
                                           .rearrange("p (n c) -> p n c", c=C)).then_inc(h_ready, 1)
                        act.wait_ge(projected, q + 1)
                        act.sem_inc(act_turn, 1)
                        held(stage_free[k], h0 + it + 1)
                        if stage > 0:
                            nc.scalar.copy(start_ring[:, k, :], start_ids[:, bass.ds((2 * it + k) * GN, GN)])
                        else:
                            for out_, a, b in ((tst[k], 0, ROW), (ast[k], ROW, ROW + C)):
                                nc.scalar.copy(out_[:, 0:6, :].rearrange("p (m n) r -> p m n r", n=3), conv_p6[:, :, :, a:b])
                                last = nc.scalar.copy(out_[:, 6, :], pP[:, 2, a:b])
                            last.then_inc(staged, 1)
                            continue
                        nc.scalar.copy(tst[k], pP[:, 0, 0:GN * ROW].rearrange("p (n r) -> p n r", r=ROW)).then_inc(staged, 1)

            def deviation(i):
                act.wait_ge(var_ready, i + 1)
                nc.scalar.activation(var[:, :], var[:, :], ACT.Sqrt).then_inc(dev_ready, 1)

            def tails(t):
                act.wait_ge(tail_in, 2 * t + 1)
                nc.scalar.activation(tail_row[:, :, :], tail_row[:, :, :], ACT.Exp).then_inc(tail_exp, 1)
                act.wait_ge(tail_in, 2 * t + 2)
                nc.scalar.activation(pexp[:, :, :], pexp[:, :, :], ACT.Exp).then_inc(tail_exp, 1)

            nc.scalar.copy(hg[:, :, :], feats_pad[:, 0:GN * C].rearrange("p (n c) -> p n c", c=C)).then_inc(h_ready, 1)
            project(0, 0)
            act.wait_ge(ids_ready, 1)
            for k in range(2):
                nc.scalar.copy(start_ring[:, k, :], start_ids[:, k * GN:(k + 1) * GN]).then_inc(starts_ready, 1)
            with act.Fori(1, PAIRS) as it:
                for k in range(2):
                    held(terms_scattered[k], 16 * GN * it)
                    nc.scalar.copy(start_ring[:, k, :], start_ids[:, bass.ds((2 * it + k) * GN, GN)]).then_inc(starts_ready, 1)
            with act.Fori(0, CHUNKS) as c:
                act.wait_ge(ein_loaded, 16 * (c + 1))
                act.sem_inc(act_turn, 1)
                held(X_free, c + 1)
                nc.scalar.copy(F3[:, 0:C, 1:J1], keep[:, None, bass.ds(c * J, J)].to_broadcast([P, C, J]))
                nc.scalar.copy(X3[:, 0:C, 1:J1], ein_jc.rearrange("p j c -> p c j")).then_inc(X_ready, 1)
                act.drain().then_inc(ein_free, 1)

            act.wait_ge(bn_ready, 1)
            nc.scalar.activation(part[:, 0, :], part[:, 0, :], ACT.Sqrt).then_inc(dev_ready, 1)
            def decay(c, k):
                held(conv_sum, c + 1)
                nc.scalar.copy(conv_f[k].rearrange("p (c j) -> p c j", j=J1)[:, :, 1:J1],
                               keep[:, None, bass.ds(c * J, J)].to_broadcast([P, SW, J])).then_inc(conv_F, 1)

            def stage_sums(c, k):
                act.wait_ge(conv_sum, c + 3)
                act.sem_inc(act_turn, 1)
                act.wait_ge(sums_free, c + 1)
                nc.scalar.copy(conv_st[k][:, :, 0:SW],
                               conv_s[k].rearrange("p (c j) -> p j c", j=J1)[:, 1:J1, :]).then_inc(rows_staged, 1)

            act.wait_ge(conv_ready, 1)
            decay(0, 0)
            with act.Fori(0, CHUNKS // 2) as it:
                for k in range(2):
                    decay(2 * it + k + 1, 1 - k)
                    stage_sums(2 * it + k, k)
            stage_sums(CHUNKS - 1, 0)

            def gat_pass(L):
                with act.Fori(0, ITER) as it:
                    for b in range(SLOTS):
                        K = L * CHUNKS + it * SLOTS + b
                        act.wait_ge(exps_in, K + 1)
                        for h in range(H):
                            nc.scalar.activation(F4[:, h, :, 1:J1],
                                                 exps[:, 0, h, None, :].to_broadcast([P, CH + 1, J]), ACT.Exp)
                        nc.scalar.activation(X4[:, :, CH, 1:J1], exps[:, 1, :, :], ACT.Exp).then_inc(weights_ready, 1)
                        act.wait_ge(gat_sum, K + 1)
                        act.sem_inc(act_turn, 1)
                        act.wait_ge(sums_free, CHUNKS + K + 2)
                        nc.scalar.copy(stage_rows[:, :, SW:ROW], run_max[:, :, 1:J1].rearrange("p h j -> p j h"))
                        nc.scalar.copy(stage_rows[:, :, 0:SW], S3[:, :, 1:J1].rearrange("p c j -> p j c")).then_inc(rows_staged, 1)
            tails(0)
            project(1, PAIRS)
            gat_pass(0)
            with act.Fori(1, LAYERS) as L:
                tails(L)
                project(2, (L + 1) * PAIRS)
                gat_pass(L)
            tails(LAYERS)
            with act.Fori(0, GROUPS) as g:
                deviation(GROUPS + g)

        @block.tensor
        def _(pe):
            pe.wait_ge(in_w0, 64)
            pe.wait_ge(consts_ready, 1)
            for k in range(2):
                last = nc.tensor.transpose(pT[0:C, 0, k * C:(k + 1) * C], w0[:, k * C:(k + 1) * C], ident[0:C, 0:C])
            last.then_inc(w0_T, 1)
            pe.sem_inc(h_T, 1)

            pe.wait_ge(hot_ready, 1)
            for t in range(BPP):
                last = nc.tensor.matmul(pS[:, 0:NPP], hot_p[:, t, :], hot_i[:, t, :], start=(t == 0), stop=(t == BPP - 1))
            last.then_inc(hist_ready, 1)
            pe.wait_ge(totals_ready, 1)
            nc.tensor.matmul(pS[:, 128:129], tri[:, :], hist[:, NPP:NPP + 1], start=True, stop=True).then_inc(before_ready, 1)
            pe.wait_ge(flag_ready, 1)
            nc.tensor.transpose(pR[0:SW, 0:P], ends[:, 0, :], ident[:, :]).then_inc(flag_T, 1)

            def project(stage, h0):
                with pe.Fori(0, PAIRS) as it:
                    for k in range(2):
                        q = 2 * (h0 + it) + k
                        pe.wait_ge(h_ready, q + 1 + (stage > 0))
                        pe.sem_inc(pe_turn, 1)
                        for n in range(GN):
                            last = nc.tensor.transpose(pT[0:C, n // 4, (n % 4) * P:(n % 4 + 1) * P], hg[:, n, :], ident[:, :])
                        last.then_inc(h_T, 1)
                        pe.wait_ge(staged, q + 1)
                        pe.sem_inc(pe_turn, 1)
                        pe.wait_ge(hT_ready, q + 1)
                        for n in range(GN):
                            lhsT = hT[:, n * P:(n + 1) * P]
                            if stage == 0:
                                o = (n % 3) * (ROW + C)
                                last = nc.tensor.matmul(pP[:, n // 3, o:o + ROW + C], lhsT, rhs0[:, :], start=True, stop=True)
                            else:
                                last = nc.tensor.matmul(pP[:, 0, n * ROW:(n + 1) * ROW], lhsT, wl[:, :], start=True, stop=True)
                        last.then_inc(projected, 1)

            def tails(t):
                pe.wait_ge(ends_ready, t + 1)
                pe.sem_inc(pe_turn, 1)
                for k in range(2):
                    last = nc.tensor.transpose(pR[0:SW, k * P:(k + 1) * P], ends[:, k, :], ident[:, :])
                last.then_inc(ends_T, 1)
                pe.wait_ge(carry_ready, t + 1)
                pe.sem_inc(pe_turn, 1)
                nc.tensor.transpose(pB[:, 0:SW], sum_row[:, 0:P], ident[0:SW, 0:SW])
                nc.tensor.transpose(pB[:, P:P + SW], max_row[:, 0:P], ident[0:SW, 0:SW]).then_inc(carry_T, 1)

            pe.wait_ge(w0_ready, 1)
            project(0, 0)
            pe.wait_ge(stat_ready, 1)
            nc.tensor.matmul(pS[:, 0:2 * C], ones[:, :], stat[:, :, :].rearrange("p a c -> p (a c)"),
                             start=True, stop=True).then_inc(stat_summed, 1)
            with pe.Fori(0, LAYERS) as L:
                tails(L)
                project(1, (L + 1) * PAIRS)
            tails(LAYERS)

        @block.vector
        def _(dve):
            v = nc.vector

            def bc(ap, shape):
                return ap.to_broadcast(shape)

            v.memset(z[:, :], 0.0).then_inc(zeros_ready, 1)
            v.memset(prev_i[:, :], -1)
            v.memset(feats[96:P, LASTN:NPP, :], 0.0)
            v.memset(feats_pad[:, NPP * C:], 0.0)
            dve.drain().then_inc(clears_done, 1)
            v.memset(ones[:, :], 1.0)
            dve.wait_ge(in_dst, 16)
            v.tensor_copy(D, dst_i)
            dve.drain()
            v.tensor_copy(first_ids[:, :], D[:, 0:1])
            dve.wait_ge(consts_ready, 1)
            v.tensor_copy(query[:, :], qi[:, :])
            v.tensor_copy(steps[:, :], step_i[:, :])
            dve.drain()

            firsts = D[:, 0:EPP:BL]
            for lo, hi in ((0, BPP // 2), (BPP // 2, BPP)):
                n = hi - lo
                w = wide[lo > 0][:, 0:n * P].rearrange("p (t q) -> p t q", q=P)
                v.tensor_tensor(w, firsts[:, lo:hi, None].to_broadcast([P, n, P]),
                                steps[:, None, :].to_broadcast([P, n, P]), ALU.is_ge)
                dve.drain()
                v.tensor_reduce(owner[:, lo:hi], w, AX, ALU.add)
            dve.drain()
            v.tensor_scalar(owner[:, :], owner[:, :], -1.0, float(NPP), ALU.add, ALU.mult)
            dve.drain()
            v.tensor_tensor(within[:, :], firsts, owner[:, :], ALU.subtract)
            v.tensor_tensor(hot_p, owner[:, :, None].to_broadcast([P, BPP, P]),
                            steps[:, None, :].to_broadcast([P, BPP, P]), ALU.is_equal)
            dve.drain()
            v.tensor_scalar(places[:, :], query[:, 1:NPP + 1], query[:, 1:2], None, ALU.subtract)
            dve.drain()
            v.tensor_tensor(hot_i, within[:, :, None].to_broadcast([P, BPP, NPP]),
                            places[:, None, :].to_broadcast([P, BPP, NPP]), ALU.is_equal).then_inc(hot_ready, 1)
            dve.wait_ge(in_w0, 64)
            v.tensor_scalar(sign[:, :], gammab[:, :], 0.0, None, ALU.is_ge)
            dve.drain()
            v.tensor_scalar(sign[:, :], sign[:, :], 2.0, 1.0, ALU.mult, ALU.subtract)
            dve.drain()
            dve.wait_ge(w0_T, 1)
            v.tensor_tensor(rhs0[:, 0:C], pT[0:C, 0, C:2 * C], sign[0:C, :], ALU.mult)
            v.tensor_tensor(rhs0[:, ROW:ROW + C], pT[0:C, 0, 0:C], sign[0:C, :], ALU.mult)
            v.memset(rhs0[:, C:ROW], 0.0)
            dve.drain()
            v.tensor_tensor(rhs0[:, ROW:ROW + C], rhs0[:, ROW:ROW + C], rhs0[:, 0:C], ALU.subtract).then_inc(w0_ready, 1)
            v.memset(hist[:, 0:1], 0.0)
            v.memset(has[:, :], 1.0)
            dve.drain()
            dve.wait_ge(hist_ready, 1)
            v.tensor_tensor_scan(hist[:, 1:NPP + 1], has[:, :], pS[:, 0:NPP], 0.0, ALU.mult, ALU.add).then_inc(totals_ready, 1)
            dve.wait_ge(before_ready, 1)
            v.tensor_copy(before[:, :], pS[:, 128:129])
            v.memset(blk[:, NPP + 1:], 0.0)
            dve.drain()
            v.tensor_scalar(blk[:, 0:NPP + 1], hist[:, :], before[:, 0:1], 1.0, ALU.add, ALU.subtract)
            dve.drain()
            v.tensor_scalar(blk[:, 0:NPP + 1], blk[:, 0:NPP + 1], 0.0, None, ALU.max)
            dve.drain()
            for k in range(QS):
                v.tensor_copy(blk_i[:, k * QB:(k + 1) * QB], blk[:, k * QB:(k + 1) * QB]).then_inc(search_ready, 1)

            v.tensor_tensor(keep[:, 1:EPP], D[:, 1:EPP], D[:, 0:EPP - 1], ALU.is_equal)
            v.memset(keep[:, 0:1], 0.0)
            v.tensor_scalar(reset[:, :], D, D[:, 0:1], None, ALU.is_equal)
            v.tensor_tensor(flags[:, 1:2], D[:, 0:1], D[:, EPP - 1:EPP], ALU.is_equal)
            dve.wait_ge(in_prev, 16)
            v.tensor_copy(flags[:, 4:5], prev_i[:, :])
            dve.drain()
            v.tensor_tensor(flags[:, 0:1], D[:, 0:1], flags[:, 4:5], ALU.is_equal)
            v.tensor_reduce(flags[:, 2:3], reset[:, :], AX, ALU.add)
            dve.drain()
            v.tensor_tensor(flags[:, 3:4], flags[:, 0:1], flags[:, 1:2], ALU.mult)
            v.tensor_scalar(reset[:, :], keep[:, :], BIG, BIG, ALU.mult, ALU.subtract)
            v.tensor_copy(flags[:, 5:6], edge0[:, :])
            dve.drain()
            v.scalar_tensor_tensor(flags[:, 4:5], flags[:, 2:3], -1.0, flags[:, 5:6], ALU.add, ALU.add)
            v.tensor_scalar(flags[:, 3:4], flags[:, 3:4], BIG, BIG, ALU.mult, ALU.subtract)
            v.tensor_scalar(flags[:, 0:1], flags[:, 0:1], BIG, BIG, ALU.mult, ALU.subtract)
            dve.drain()
            v.tensor_copy(patch_ids[:, :], flags[:, 4:5])

            dve.wait_ge(in_src, 32)
            v.tensor_copy(ring_ids[:, :], src_ids[:, 0:JI]).then_inc(slot_ready, SLOTS)
            v.tensor_copy(ends[:, 0, :], bc(flags[:, 3:4], [P, SW])).then_inc(flag_ready, 1)
            with dve.Fori(0, (NPP + 1) // QN) as it:
                for k in range(QS):
                    my = slice(k * QB, (k + 1) * QB)
                    dve.wait_ge(searched[k], 16 * QB * (it + 1))
                    v.tensor_copy(got_f, got[k])
                    dve.drain()
                    v.tensor_tensor(cmp_b, query[:, bass.ds(it * QN + k * QB, QB)][:, :, None].to_broadcast([P, QB, BL]),
                                    got_f, ALU.is_ge)
                    v.tensor_copy(blk_i[:, my], blk[:, bass.ds((it + 1) * QN + k * QB, QB)]).then_inc(search_ready, 1)
                    dve.drain()
                    v.tensor_reduce(cnt[:, :], cmp_b, AX, ALU.add)
                    dve.drain()
                    v.scalar_tensor_tensor(count[:, bass.ds(it * QN + k * QB, QB)], blk[:, bass.ds(it * QN + k * QB, QB)],
                                           float(BL), cnt[:, :], ALU.mult, ALU.add)
                    dve.drain()
            dve.drain().then_inc(search_done, 1)
            v.tensor_tensor(has[:, :], count[:, 1:NPP + 1], count[:, 0:NPP], ALU.is_gt)
            v.tensor_scalar(tmp_end[:, :], count[:, 1:NPP + 1], -1.0, 0.0, ALU.add, ALU.max)
            v.tensor_scalar(tmp_none[:, :], query[:, 1:NPP + 1], float(E), None, ALU.add)
            dve.drain()
            v.memset(end_ids[:, NPP:NPP + 2 * GN], 0.0)
            v.tensor_copy(end_ids[:, 0:NPP], tmp_end[:, :])
            v.tensor_tensor(tmp_start[:, :], count[:, 0:NPP], tmp_none[:, :], ALU.subtract)
            dve.drain()
            v.tensor_tensor(tmp_start[:, :], tmp_start[:, :], has[:, :], ALU.mult)
            dve.drain()
            v.tensor_tensor(tmp_start[:, :], tmp_start[:, :], tmp_none[:, :], ALU.add)
            dve.drain()
            v.tensor_copy(start_ids[:, :], tmp_start[:, :]).then_inc(ids_ready, 1)

            dve.wait_ge(flag_T, 1)
            v.tensor_copy(reset_row[:, :], pR[0:SW, 0:P])
            dve.wait_ge(in_w, 16 * 5 * LAYERS)
            v.tensor_tensor(asb[:, :, :], ws[:, :, :], asb[:, :, :], ALU.mult)
            v.tensor_tensor(adb[:, :, :], wd[:, :, :], adb[:, :, :], ALU.mult)
            v.tensor_copy(wcat[:, :, 0:C], ws[:, :, :])
            dve.drain()
            v.tensor_reduce(wcat[:, :, C:C + 2], asb[:, :, :].rearrange("k l (h c) -> k l h c", h=H), AX, ALU.add)
            v.tensor_reduce(wcat[:, :, C + 2:ROW], adb[:, :, :].rearrange("k l (h c) -> k l h c", h=H), AX, ALU.add)

            for buf in (X, F, S, max_row, sum_row):
                v.memset(buf[:, :], 0.0)
            for buf in (run_max, alpha_e, stat):
                v.memset(buf[:, :, :], 0.0)
            v.memset(stage_rows[:, :, :], 0.0)
            dve.drain().then_inc(X_free, 1)

            with dve.Fori(0, ITER) as it:
                for b in range(SLOTS):
                    c = it * SLOTS + b
                    dve.wait_ge(X_ready, c + 1)
                    v.tensor_copy(X3[:, 0:C, 0:1], S3[:, 0:C, J:J1])
                    dve.drain()
                    v.tensor_tensor_scan(S[:, 0:C * J1], F[:, 0:C * J1], X[:, 0:C * J1], 0.0, ALU.mult, ALU.add)\
                        .then_inc(X_free, 1)
                    dve.drain()
                    dve.wait_ge(conv_gathered[b], ONE_STEP * (it + 1))
                    dve.sem_inc(dve_turn, 1)
                    dve.wait_ge(z_free, c + 1)
                    v.tensor_tensor(z3, S3[:, 0:C, 1:J1], slot_rows[:, b, :, 0:C].rearrange("p j c -> p c j"),
                                    ALU.add).then_inc(z_ready, 1)
                    dve.drain()
                    v.tensor_copy(ring_ids[:, b * J:(b + 1) * J], src_ids[:, bass.ds((it + 1) * JI + b * J, J)])\
                        .then_inc(slot_ready, 1)
                    v.tensor_tensor(z2[:, :], z[:, :], z[:, :], ALU.mult)
                    v.tensor_reduce(part[:, 0, :], z3, AX, ALU.add)
                    dve.drain()
                    v.tensor_reduce(part[:, 1, :], z23, AX, ALU.add)
                    dve.drain()
                    v.tensor_tensor(stat[:, :, :], stat[:, :, :], part[:, :, :], ALU.add)
            dve.drain().then_inc(stat_ready, 1)

            dve.wait_ge(stat_summed, 1)
            v.tensor_scalar(bn[:, :, :].rearrange("p a c -> p (a c)"), pS[:, 0:2 * C], 1.0 / E, None, ALU.mult)
            v.tensor_tensor(b0b[:, :], b0b[:, :], sign[:, :], ALU.mult)
            v.tensor_tensor(gammab[:, :], gammab[:, :], sign[:, :], ALU.mult)
            dve.drain()
            v.tensor_tensor(part[:, 0, :], bn[:, 0, :], bn[:, 0, :], ALU.mult)
            v.tensor_tensor(part[:, 1, :], bn[:, 0, :], b0b[:, :], ALU.add)
            dve.drain()
            v.tensor_tensor(part[:, 0, :], bn[:, 1, :], part[:, 0, :], ALU.subtract)
            v.tensor_tensor(part[:, 1, :], b0b[:, :], part[:, 1, :], ALU.subtract)
            dve.drain()
            v.tensor_scalar(part[:, 0, :], part[:, 0, :], 0.0, BN_EPS, ALU.max, ALU.add)
            dve.drain().then_inc(bn_ready, 1)
            dve.wait_ge(dev_ready, 1)
            v.reciprocal(part[:, 0, :], part[:, 0, :])
            dve.drain()
            v.tensor_tensor(bn_s[:, :], part[:, 0, :], gammab[:, :], ALU.mult)
            dve.drain()
            v.tensor_scalar(bn_s[:, :], bn_s[:, :], TINY, None, ALU.max)
            dve.drain()
            v.reciprocal(part[:, 0, :], bn_s[:, :])
            dve.drain()
            v.tensor_tensor(part[:, 0, :], part[:, 0, :], betab[:, :], ALU.mult)
            dve.drain()
            v.tensor_tensor(bn_t[:, :], part[:, 1, :], part[:, 0, :], ALU.add)
            for buf in (F2, S2):
                v.memset(buf, 0.0)
            v.memset(stage2, 0.0)
            for buf in conv_x:
                v.memset(buf.rearrange("p (h c j) -> p h c j", h=H, j=J1)[:, :, CH, :], 1.0)
            dve.drain().then_inc(conv_ready, 1)
            dve.sem_inc(conv_sum, 2)
            dve.sem_inc(conv_u_free, 2)

            def conv_step(c, k):
                xk, other = conv_x[k], conv_s[1 - k]
                x4 = xk.rearrange("p (h c j) -> p h c j", h=H, j=J1)
                u3 = conv_u[k].rearrange("p (c j) -> p c j", j=J)
                v.tensor_copy(xk.rearrange("p (c j) -> p c j", j=J1)[:, :, 0:1],
                              other.rearrange("p (c j) -> p c j", j=J1)[:, :, J:J1])
                dve.wait_ge(shifted, c + 1)
                for h in range(H):
                    uh = u3[:, h * CH:(h + 1) * CH, :]
                    last = v.scalar_tensor_tensor(x4[:, h, 0:CH, 1:J1], uh, SLOPE0, uh, ALU.mult, ALU.max)
                last.then_inc(conv_u_free, 1)
                dve.drain()
                dve.wait_ge(rows_staged, c + 1)
                dve.sem_inc(dve_turn, 1)
                dve.wait_ge(conv_F, c + 1)
                v.tensor_tensor_scan(conv_s[k], conv_f[k], xk, 0.0, ALU.mult, ALU.add).then_inc(conv_sum, 1)
                dve.drain()

            with dve.Fori(0, CHUNKS // 2) as it:
                for k in range(2):
                    conv_step(2 * it + k, k)
            conv_step(CHUNKS - 1, 0)
            dve.wait_ge(rows_staged, CHUNKS + 2)
            dve.sem_inc(dve_turn, 1)

            def complete_first_rows(t):
                last_row = stage_rows[:, J - 1, :]
                v.tensor_copy(ends[:, 0, :], last_row[:, 0:SW])
                for h in range(H):
                    last = v.tensor_copy(ends[:, 1, h * (CH + 1):(h + 1) * (CH + 1)],
                                         bc(last_row[:, SW + h:SW + h + 1], [P, CH + 1]))
                last.then_inc(ends_ready, 1)
                dve.wait_ge(ends_T, t + 1)
                v.tensor_tensor_scan(max_row[:, 1:P + 1], reset_row[:, :], pR[0:SW, P:2 * P], 0.0, ALU.add, ALU.max)
                dve.drain()
                v.tensor_tensor(tail_row[:, 0, :], max_row[:, 0:P], reset_row[:, :], ALU.add)
                v.tensor_tensor(tail_row[:, 1, :], pR[0:SW, P:2 * P], max_row[:, 1:P + 1], ALU.subtract)
                dve.drain()
                v.tensor_tensor(tail_row[:, 0, :], tail_row[:, 0, :], max_row[:, 1:P + 1], ALU.subtract).then_inc(tail_in, 1)
                dve.wait_ge(tail_exp, 2 * t + 1)
                v.tensor_tensor(tail_row[:, 1, :], tail_row[:, 1, :], pR[0:SW, 0:P], ALU.mult)
                dve.drain()
                v.tensor_tensor_scan(sum_row[:, 1:P + 1], tail_row[:, 0, :], tail_row[:, 1, :], 0.0, ALU.mult, ALU.add)\
                    .then_inc(carry_ready, 1)
                dve.wait_ge(patch_gathered, 16 * (t + 1))
                for h in range(H):
                    v.tensor_copy(pmax[:, 0, h * (CH + 1):(h + 1) * (CH + 1)],
                                  bc(patch[:, SW + h:SW + h + 1], [P, CH + 1]))
                dve.wait_ge(carry_T, t + 1)
                v.tensor_scalar(pmax[:, 1, :], pB[:, P:P + SW], flags[:, 0:1], None, ALU.add)
                dve.drain()
                v.tensor_tensor(pmax[:, 2, :], pmax[:, 0, :], pmax[:, 1, :], ALU.max)
                dve.drain()
                v.tensor_tensor(pexp[:, 0, :], pmax[:, 0, :], pmax[:, 2, :], ALU.subtract)
                v.tensor_tensor(pexp[:, 1, :], pmax[:, 1, :], pmax[:, 2, :], ALU.subtract).then_inc(tail_in, 1)
                dve.wait_ge(tail_exp, 2 * t + 2)
                v.tensor_tensor(pexp[:, 0, :], pexp[:, 0, :], patch[:, 0:SW], ALU.mult)
                v.tensor_tensor(pexp[:, 1, :], pexp[:, 1, :], pB[:, 0:SW], ALU.mult)
                dve.drain()
                v.tensor_tensor(patch[:, 0:SW], pexp[:, 0, :], pexp[:, 1, :], ALU.add).then_inc(patch_ready, 1)

            def put_ids(g, k):
                v.tensor_copy(end_ring[:, k, :], end_ids[:, bass.ds(g * GN, GN)]).then_inc(node_ids, 1)

            def node_means(t, it, k, q):
                g = 2 * it + k
                dve.drain()
                dve.wait_ge(nodes_fetched[k], 16 * GN * (t * PAIRS + it + 1))
                r = node4[k][:, :, 0:SW].rearrange("p n (h c) -> p n h c", h=H)
                v.reciprocal(rden[:, :, :], r[:, :, :, CH])
                dve.drain()
                v.tensor_tensor(rden[:, :, :], rden[:, :, :],
                                has[:, bass.ds(g * GN, GN)][:, :, None].to_broadcast([P, GN, H]), ALU.mult)
                dve.drain()
                if q is not None:
                    dve.wait_ge(h_T, q + 1)
                    dve.sem_inc(dve_turn, 1)
                v.tensor_tensor(hg2[:, :, :].rearrange("p n (h c) -> p n h c", h=H), r[:, :, :, 0:CH],
                                rden[:, :, :, None].to_broadcast([P, GN, H, CH]), ALU.mult)
                dve.drain()
                put_ids(g + 2, k)

            def layer_norm(g, i, target):
                mine = feats[:, bass.ds(g * GN, GN), :]
                v.tensor_tensor(hg2[:, :, :], hg2[:, :, :], mine, ALU.add)
                dve.drain()
                v.tensor_reduce(mean[:, :], hg2[:, :, :], AX, ALU.add)
                dve.drain()
                v.tensor_scalar(mean[:, :], mean[:, :], 1.0 / C, None, ALU.mult)
                dve.drain()
                v.tensor_tensor(hg2[:, :, :], hg2[:, :, :], mean[:, :, None].to_broadcast([P, GN, C]), ALU.subtract)
                dve.drain()
                v.tensor_tensor(sq[:, :, :], hg2[:, :, :], hg2[:, :, :], ALU.mult)
                dve.drain()
                v.tensor_reduce(var[:, :], sq[:, :, :], AX, ALU.add)
                dve.drain()
                v.tensor_scalar(var[:, :], var[:, :], 1.0 / C, LN_EPS, ALU.mult, ALU.add).then_inc(var_ready, 1)
                dve.wait_ge(dev_ready, i + 2)
                v.reciprocal(var[:, :], var[:, :])
                dve.drain()
                return v.tensor_tensor(target if target is not None else mine, hg2[:, :, :],
                                       var[:, :, None].to_broadcast([P, GN, C]), ALU.mult)

            def gat_pass(L):
                with dve.Fori(0, ITER) as it:
                    dve.drain()
                    dve.wait_ge(alpha_loaded, 16 * (L * ITER + it + 1))
                    v.tensor_copy(alpha_e[:, :, 0:1], alpha_e[:, :, JI:JI + 1])
                    dve.drain()
                    for h in range(H):
                        last = v.tensor_tensor_scan(alpha_e[:, h, 1:JI + 1], keep[:, bass.ds(it * JI, JI)],
                                                    alpha_raw[:, :, h], alpha_e[:, h, 0:1], ALU.mult, ALU.add)
                    last.then_inc(alpha_free, 1)
                    dve.drain()
                    for b in range(SLOTS):
                        K = L * CHUNKS + it * SLOTS + b
                        dve.wait_ge(gat_gathered[b], ONE_STEP * (L * ITER + it + 1))
                        v.tensor_tensor(logit0[:, :, :], slot_rows[:, b, :, C:C + 2].rearrange("p j h -> p h j"),
                                        alpha_e[:, :, 1 + b * J:1 + (b + 1) * J], ALU.add)
                        dve.drain()
                        v.scalar_tensor_tensor(logit[:, :, :], logit0[:, :, :], SLOPE1, logit0[:, :, :], ALU.mult, ALU.max)
                        dve.wait_ge(rows_staged, CHUNKS + K + 2)
                        dve.sem_inc(dve_turn, 1)
                        v.tensor_copy(run_max[:, :, 0:1], run_max[:, :, J:J1])
                        v.tensor_copy(X3[:, :, 0:1], S3[:, :, J:J1])
                        dve.drain()
                        mask = reset[:, bass.ds(it * JI + b * J, J)]
                        for h in range(H):
                            v.tensor_tensor_scan(run_max[:, h, 1:J1], mask, logit[:, h, :], run_max[:, h, 0:1],
                                                 ALU.add, ALU.max)
                        dve.drain()
                        v.tensor_tensor(exps[:, 0, :, :], run_max[:, :, 0:J],
                                        mask[:, None, :].to_broadcast([P, H, J]), ALU.add)
                        v.tensor_tensor(exps[:, 1, :, :], logit[:, :, :], run_max[:, :, 1:J1], ALU.subtract)
                        dve.drain()
                        v.tensor_tensor(exps[:, 0, :, :], exps[:, 0, :, :], run_max[:, :, 1:J1], ALU.subtract)\
                            .then_inc(exps_in, 1)
                        dve.wait_ge(weights_ready, K + 1)
                        v.tensor_tensor(X4[:, :, 0:CH, 1:J1],
                                        slot_rows[:, b, :, 0:C].rearrange("p j (h c) -> p h c j", h=H),
                                        X4[:, :, CH:CH + 1, 1:J1].to_broadcast([P, H, CH, J]), ALU.mult)
                        dve.drain()
                        v.tensor_tensor_scan(S[:, :], F[:, :], X[:, :], 0.0, ALU.mult, ALU.add).then_inc(gat_sum, 1)
                        v.tensor_copy(ring_ids[:, b * J:(b + 1) * J], src_ids[:, bass.ds((it + 1) * JI + b * J, J)])\
                            .then_inc(slot_ready, 1)
                dve.drain()
                dve.wait_ge(rows_staged, (L + 2) * CHUNKS + 2)
                dve.sem_inc(dve_turn, 1)

            def node_groups(t, finish):
                dve.drain()
                for k in range(2):
                    put_ids(k, k)
                with dve.Fori(0, PAIRS) as it:
                    for k in range(2):
                        finish(it, k)

            def after_conv(it, k):
                q = GROUPS + 2 * it + k
                node_means(0, it, k, q)
                v.tensor_tensor(hg2[:, :, :], hg2[:, :, :], bn_s[:, None, :].to_broadcast([P, GN, C]), ALU.mult)
                dve.drain()
                layer_norm(2 * it + k, 2 * it + k, hg[:, :, :])
                dve.drain()
                v.tensor_copy(feats[:, bass.ds((2 * it + k) * GN, GN), :], hg[:, :, :]).then_inc(h_ready, 1)

            complete_first_rows(0)
            v.tensor_copy(wl[:, :], wcat[:, 0, :])
            node_groups(0, after_conv)
            gat_pass(0)

            with dve.Fori(1, LAYERS) as L:
                complete_first_rows(L)
                v.tensor_copy(wl[:, :], wcat[:, bass.ds(L, 1), :].rearrange("k a r -> k (a r)"))
                dve.drain()
                v.tensor_copy(bias_l[:, :], biasb[:, bass.ds(L - 1, 1), :].rearrange("p a c -> p (a c)"))

                def after_gat(it, k):
                    q = (L + 1) * GROUPS + 2 * it + k
                    node_means(L, it, k, q)
                    v.tensor_tensor(hg2[:, :, :], hg2[:, :, :], bias_l[:, None, :].to_broadcast([P, GN, C]), ALU.add)
                    dve.drain()
                    v.tensor_scalar(hg[:, :, :], hg2[:, :, :], 0.0, None, ALU.max).then_inc(h_ready, 1)

                node_groups(L, after_gat)
                gat_pass(L)

            complete_first_rows(LAYERS)

            def after_last(it, k):
                node_means(LAYERS, it, k, None)
                v.tensor_tensor(hg2[:, :, :], hg2[:, :, :], biasb[:, LAYERS - 1, None, :].to_broadcast([P, GN, C]), ALU.add)
                dve.drain()
                layer_norm(2 * it + k, GROUPS + 2 * it + k, None).then_inc(out_ready, 1)

            node_groups(LAYERS, after_last)


_WEIGHTS = ["L1_gnn_Ws", "L1_gnn_Wd", "L1_gnn_as", "L1_gnn_ad", "L1_gnn_b"]


def kernel(**inputs):
    import concourse.bacc as bacc
    from concourse.bass_utils import run_bass_kernel_spmd as run

    nc = bacc.Bacc("TRN2", target_bir_lowering=False, num_devices=1)
    arrays = {}

    def given(name):
        a = np.ascontiguousarray(inputs[name])
        arrays[name] = a
        return nc.dram_tensor(name, a.shape, mybir.dt.from_np(a.dtype), kind="ExternalInput").ap()

    first = [given(n) for n in ("x", "src", "dst", "L0_gnn_W", "L0_gnn_b", "L0_gnn_gamma", "L0_gnn_beta")]
    layers = [[given(f"{n}{l + 1}") for l in range(LAYERS)] for n in _WEIGHTS]
    out = nc.dram_tensor("out", (N, C), mybir.dt.float32, kind="ExternalOutput").ap()
    build(nc, *first, *layers, out)
    return run(nc, [arrays], core_ids=[0]).results[0]["out"]
```
